# Optimizing a Trainium2 kernel written in Bass

```python
import numpy as np
import jax
import jax.numpy as jnp

def _softmax(x, axis=-1):
    return jax.nn.softmax(x, axis=axis)

def _gelu(x):
    return jax.nn.gelu(x, approximate=True)

def _silu(x):
    return jax.nn.silu(x)

def _sigmoid(x):
    return jax.nn.sigmoid(x)

def _layernorm(x, axis=-1, eps=1e-05):
    m = jnp.mean(x, axis=axis, keepdims=True)
    v = jnp.var(x, axis=axis, keepdims=True)
    return (x - m) / jnp.sqrt(v + eps)

def _scatter_add(tgt, idx, src, axis=0):
    return tgt.at[idx].add(src)

def _segment_sum(src, seg, n):
    return jax.ops.segment_sum(src, seg, n)
kernel_name = 'mk_sandwich_d1_jaxref_r8_1efdc5'

def setup_inputs(seed: int=0):
    np.random.seed(seed)
    _w = jnp.asarray

    def _L0_attn_setup():
        import jax, jax.numpy as jnp
        import numpy as np
        K_DIM = 64
        SQRT_K = float(np.sqrt(K_DIM))

        def build_metric(halves, diagonals_nk):
            H, K = diagonals_nk.shape
            iu, ju = np.triu_indices(K, k=1)
            m = jnp.zeros((H, K, K), dtype=halves.dtype).at[:, iu, ju].set(halves)
            m = m + m.transpose(0, 2, 1)
            d = np.arange(K)
            return m.at[:, d, d].set(diagonals_nk)
        key = jax.random.key(seed)
        ks = jax.random.split(key, 6)
        B, W, C, H = (2, 256, 128, 16)
        K = C // H
        return {'in_sequence_bwc': jax.random.normal(ks[0], (B, W, C), dtype=jnp.float32), 'projection_1nck': jax.random.normal(ks[1], (1, H, C, K), dtype=jnp.float32), 'halves': jax.random.normal(ks[2], (H, K * (K + 1) // 2 - K), dtype=jnp.float32), 'diagonals_nk': jax.random.normal(ks[3], (H, K), dtype=jnp.float32), 'mixer_w': jax.random.normal(ks[4], (C, C), dtype=jnp.float32), 'mixer_b': jax.random.normal(ks[5], (C,), dtype=jnp.float32)}
    _L0_attn_in = _L0_attn_setup()

    def _L0_ffn_setup():
        import jax, jax.numpy as jnp
        import numpy as np
        E = 8
        H = 128
        M = 256
        K = 2
        SE = 1
        BSZ, SEQ = (2, 128)
        W_SCALE = 0.02
        key = jax.random.key(seed)
        ks = jax.random.split(key, 9)
        return {'x': jax.random.normal(ks[0], (BSZ, SEQ, H), jnp.float32), 'gate_w': jax.random.normal(ks[1], (E, H), jnp.float32) * W_SCALE, 'beta': jnp.zeros((E,), jnp.float32), 'gate_proj_w': jax.random.normal(ks[2], (E, H, M), jnp.float32) * W_SCALE, 'up_proj_w': jax.random.normal(ks[3], (E, H, M), jnp.float32) * W_SCALE, 'down_proj_w': jax.random.normal(ks[4], (E, M, H), jnp.float32) * W_SCALE, 'shared_gate_w': jax.random.normal(ks[5], (SE, H, M), jnp.float32) * W_SCALE, 'shared_up_w': jax.random.normal(ks[6], (SE, H, M), jnp.float32) * W_SCALE, 'shared_down_w': jax.random.normal(ks[7], (SE, M, H), jnp.float32) * W_SCALE}
    _L0_ffn_in = _L0_ffn_setup()
    _d = {'L0_attn_in_sequence_bwc': _L0_attn_in['in_sequence_bwc'], 'L0_attn_projection_1nck': _L0_attn_in['projection_1nck'], 'L0_attn_halves': _L0_attn_in['halves'], 'L0_attn_diagonals_nk': _L0_attn_in['diagonals_nk'], 'L0_attn_mixer_w': _L0_attn_in['mixer_w'], 'L0_attn_mixer_b': _L0_attn_in['mixer_b'], 'L0_ffn_gate_w': _L0_ffn_in['gate_w'], 'L0_ffn_beta': _L0_ffn_in['beta'], 'L0_ffn_gate_proj_w': _L0_ffn_in['gate_proj_w'], 'L0_ffn_up_proj_w': _L0_ffn_in['up_proj_w'], 'L0_ffn_down_proj_w': _L0_ffn_in['down_proj_w'], 'L0_ffn_shared_gate_w': _L0_ffn_in['shared_gate_w'], 'L0_ffn_shared_up_w': _L0_ffn_in['shared_up_w'], 'L0_ffn_shared_down_w': _L0_ffn_in['shared_down_w']}
    _x0 = _d['L0_attn_in_sequence_bwc']
    _d['L0_attn_in_sequence_bwc'] = jax.random.normal(jax.random.fold_in(jax.random.key(seed), 1), (2, 2048, 128), dtype=_x0.dtype)
    del _x0
    return _d

def reference(L0_attn_in_sequence_bwc, L0_attn_projection_1nck, L0_attn_halves, L0_attn_diagonals_nk, L0_attn_mixer_w, L0_attn_mixer_b, L0_ffn_gate_w, L0_ffn_beta, L0_ffn_gate_proj_w, L0_ffn_up_proj_w, L0_ffn_down_proj_w, L0_ffn_shared_gate_w, L0_ffn_shared_up_w, L0_ffn_shared_down_w):

    def _L0_attn_ref(in_sequence_bwc, projection_1nck, halves, diagonals_nk, mixer_w, mixer_b):
        import jax, jax.numpy as jnp
        import numpy as np
        K_DIM = 64
        SQRT_K = float(np.sqrt(K_DIM))

        def build_metric(halves, diagonals_nk):
            H, K = diagonals_nk.shape
            iu, ju = np.triu_indices(K, k=1)
            m = jnp.zeros((H, K, K), dtype=halves.dtype).at[:, iu, ju].set(halves)
            m = m + m.transpose(0, 2, 1)
            d = np.arange(K)
            return m.at[:, d, d].set(diagonals_nk)
        B, W, C = in_sequence_bwc.shape
        metric_nkk = build_metric(halves, diagonals_nk)
        proj_nck = projection_1nck[0]
        proj_bnwk = jnp.einsum('bwc,nck->bnwk', in_sequence_bwc, proj_nck)
        pm_bnwk = jnp.einsum('bnwk,nkl->bnwl', proj_bnwk, metric_nkk)
        dots_bnww = jnp.einsum('bnwl,bnvl->bnwv', pm_bnwk, proj_bnwk)
        nudged_bnwk = jnp.einsum('bnwv,bnvk->bnwk', dots_bnww, proj_bnwk)
        nudged_bwc = nudged_bnwk.transpose(0, 2, 1, 3).reshape(B, W, C)
        return nudged_bwc @ mixer_w.T + mixer_b

    def _L0_ffn_ref(x, gate_w, beta, gate_proj_w, up_proj_w, down_proj_w, shared_gate_w, shared_up_w, shared_down_w):
        import jax, jax.numpy as jnp
        import numpy as np
        E = 8
        H = 128
        M = 256
        K = 2
        SE = 1
        BSZ, SEQ = (2, 128)
        W_SCALE = 0.02
        B0, S0, H0 = x.shape
        xt = x.reshape(-1, H0)
        B = xt.shape[0]
        logits = xt @ gate_w.T
        _, idx = jax.lax.top_k(logits + beta, K)
        probs = jax.nn.sigmoid(jnp.take_along_axis(logits, idx, axis=-1))
        c = jnp.zeros((B, E), xt.dtype).at[jnp.arange(B)[:, None], idx].add(probs)
        g = jnp.einsum('bh,ehm->bem', xt, gate_proj_w)
        u = jnp.einsum('bh,ehm->bem', xt, up_proj_w)
        h = jax.nn.silu(g) * u
        eo = jnp.einsum('bem,emh->beh', h, down_proj_w)
        combined = jnp.einsum('beh,be->bh', eo, c)
        sg = jnp.einsum('bh,ehm->bem', xt, shared_gate_w)
        su = jnp.einsum('bh,ehm->bem', xt, shared_up_w)
        sh = jax.nn.silu(sg) * su
        shared_out = jnp.einsum('bem,emh->beh', sh, shared_down_w).sum(axis=1)
        return (combined + shared_out).reshape(B0, S0, H0)
    x = L0_attn_in_sequence_bwc
    x = x + _layernorm(_L0_attn_ref(_layernorm(x, axis=-1), L0_attn_projection_1nck, L0_attn_halves, L0_attn_diagonals_nk, L0_attn_mixer_w, L0_attn_mixer_b), axis=-1)
    x = x + _layernorm(_L0_ffn_ref(_layernorm(x, axis=-1), L0_ffn_gate_w, L0_ffn_beta, L0_ffn_gate_proj_w, L0_ffn_up_proj_w, L0_ffn_down_proj_w, L0_ffn_shared_gate_w, L0_ffn_shared_up_w, L0_ffn_shared_down_w), axis=-1)
    return x

_drawn_inputs = setup_inputs


def setup_inputs(seed=0):
    import zlib

    import numpy as np

    out = dict(_drawn_inputs(seed))
    spreads = {'L0_ffn_beta': (0.0, 0.1)}
    factors = {}
    for name, (base, spread) in spreads.items():
        noise = np.random.default_rng([zlib.crc32(name.encode()), seed]).standard_normal(out[name].shape)
        drawn = base * np.exp(spread * noise) if base else spread * noise
        out[name] = jnp.asarray(drawn.astype(out[name].dtype))
    for name, factor in factors.items():
        out[name] = (out[name] * factor).astype(out[name].dtype)
    return out
```

```python
from contextlib import ExitStack

import concourse.bass as bass
from concourse import mybir

F32 = mybir.dt.float32
F32R = mybir.dt.float32r
BF16 = mybir.dt.bfloat16
I32 = mybir.dt.int32
U32 = mybir.dt.uint32
ALU = mybir.AluOpType
ACT = mybir.ActivationFunctionType
AX = mybir.AxisListType

P = 128
G = 4
EPS = 1e-5
TOPK = 2


def build_sandwich(nc, x, proj, halves, diag, mixer_w, mixer_b, gate_w, beta,
                   wg, wu, wd, sg, su, sd, out):
    B, W, C = x.shape
    H, K = diag.shape
    E, _, M = wg.shape
    MC = M // P
    TPB = W // P
    TILES = B * TPB
    QS = TPB // G
    STEPS = B * QS
    T = B * W
    assert C == P and H * K == P and B == 2 and TOPK * M == 4 * P

    REGION = T + P
    ROW = P + 4
    EMPTY_REGION = E * REGION
    UNROLL = 8
    SLOTS = -(-((TOPK * T + E * (P - 1)) // P) // UNROLL) * UNROLL
    NOWHERE = TOPK * T

    x_v = x.rearrange("b (p j) c -> p b j c", p=P)
    out_v = out.rearrange("b (p j) c -> p b j c", p=P)

    with ExitStack() as ctx:
        def sb(name, shape, dt=F32):
            return ctx.enter_context(nc.sbuf_tensor(name, shape, dt))

        def sem(name):
            return ctx.enter_context(nc.semaphore(name))

        rows_d = nc.dram_tensor("expert_rows", [EMPTY_REGION + P, ROW], F32).ap()
        res_d = nc.dram_tensor("expert_results", [TOPK * T, C], F32).ap()
        res_v = res_d.rearrange("(k p t) c -> p k t c", k=TOPK, p=P)

        X = sb("X", [P, B, TPB, C])
        xnT = sb("xnT", [P, B, TPB * P])
        x1 = sb("x1", [P, B, TPB, C])
        ysh = sb("ysh", [P, B, TPB, C])
        ck = sb("ck", [P, B, TPB, TOPK])
        ids = sb("ids", [P, TOPK, B, TPB], I32)
        gu_f = sb("gu_f", [P, E + 1, 2 * M])
        gu_hi = sb("gu_hi", [P, E + 1, 2 * M], F32R)
        gu_lo = sb("gu_lo", [P, E + 1, 2 * M], F32R)
        down = sb("down", [P, E + 1, MC, C])
        ident = sb("ident", [P, P])
        headmask = sb("headmask", [P, H, K])
        below = sb("below", [P, P], BF16)
        ones_b = sb("ones_b", [P, P], BF16)
        iota8 = sb("iota8", [P, E])
        iota_t = sb("iota_t", [1, SLOTS])
        upto = sb("upto", [1, E, E])
        regbase = sb("regbase", [P, E])
        mhalf = sb("mhalf", [P, G])
        pidx = sb("pidx", [P, 1])
        empty_row = sb("empty_row", [P, ROW])
        Wc = sb("Wc", [P, H, K])
        WT = sb("WT", [P, P])
        mix = sb("mix", [P, C])
        mixT = sb("mixT", [P, C])
        mixb = sb("mixb", [P, 1])
        ucomp = sb("ucomp", [P, K])
        dcomp = sb("dcomp", [P, 1])
        ubig = sb("ubig", [P, P])
        udiag = sb("udiag", [P, P])
        iddiag = sb("iddiag", [P, P])
        metric = sb("metric", [P, P])
        LT = sb("LT", [P, P])
        gw = sb("gw", [E, C])
        gwT = sb("gwT", [P, E])
        gw2 = sb("gw2", [P, 2, E], F32R)
        beta_sb = sb("beta_sb", [P, E])
        S_sb = [sb(f"S_sb{b}", [P, P]) for b in range(B)]
        T1 = [sb(f"T1_{b}", [P, P]) for b in range(B)]
        Gm = [sb(f"Gm{b}", [P, P]) for b in range(B)]
        R_sb = [sb(f"R_sb{b}", [P, P]) for b in range(B)]
        A_sb = [sb(f"A_sb{b}", [P, P]) for b in range(B)]
        xn = [sb(f"xn{u}", [P, G, C]) for u in range(2)]
        st = [sb(f"st{u}", [P, G, 6]) for u in range(2)]
        mv = [sb(f"mv{u}", [P, G, 2]) for u in range(2)]
        vpe = [sb(f"vpe{u}", [P, G]) for u in range(2)]
        rstd = [sb(f"rstd{u}", [P, G]) for u in range(2)]
        nmean = [sb(f"nmean{u}", [P, G]) for u in range(2)]
        shift = [sb(f"shift{u}", [P, G]) for u in range(2)]
        st3 = [sb(f"st3{u}", [P, G, 6]) for u in range(2)]
        mv3 = [sb(f"mv3{u}", [P, G, 2]) for u in range(2)]
        vpe3 = [sb(f"vpe3{u}", [P, G]) for u in range(2)]
        rstd3 = [sb(f"rstd3{u}", [P, G]) for u in range(2)]
        outT = [sb(f"outT{u}", [P, G * P]) for u in range(2)]
        tln = [sb(f"tln{u}", [P, G, C]) for u in range(2)]
        xt = [sb(f"xt{u}", [P, G, C]) for u in range(2)]
        xh = [sb(f"xh{u}", [P, G, P], F32R) for u in range(2)]
        xl = [sb(f"xl{u}", [P, G, P], F32R) for u in range(2)]
        src = [sb(f"src{u}", [P, TOPK, G, ROW]) for u in range(2)]
        slot = [sb(f"slot{u}", [P, G, TOPK], U32) for u in range(2)]
        logits = sb("logits", [P, G, E])
        sel = sb("sel", [P, G, E])
        mx = sb("mx", [P, G, 8])
        ix = sb("ix", [P, G, 8], U32)
        ixf = sb("ixf", [P, G, TOPK])
        chosen = sb("chosen", [P, G, TOPK, E])
        picked = sb("picked", [P, G, TOPK, E])
        mask = sb("mask", [P, G + 1, E], BF16)
        th = sb("th", [P, G, E])
        sig = sb("sig", [P, G, E])
        place = sb("place", [P, G, E])
        slotf = sb("slotf", [P, G, TOPK])
        carry = sb("carry", [P, E])
        padidx_f = sb("padidx_f", [P, E])
        padidx = sb("padidx", [P, E], U32)
        cnt = sb("cnt", [1, E])
        cnti = sb("cnti", [1, E], I32)
        ntiles_i = sb("ntiles_i", [1, E], I32)
        ntiles = sb("ntiles", [1, E])
        ends8 = sb("ends8", [1, E, E])
        ends = sb("ends", [1, E])
        step_of = sb("step_of", [1, E])
        past = sb("past", [1, SLOTS, E])
        past_s = sb("past_s", [1, SLOTS, E])
        exp_f = sb("exp_f", [1, SLOTS])
        exp_i = sb("exp_i", [1, SLOTS], I32)
        row_f = sb("row_f", [1, SLOTS])
        row_g = sb("row_g", [1, SLOTS])
        row_i = sb("row_i", [1, SLOTS], I32)
        rowt = [sb(f"rowt{v}", [P, ROW]) for v in range(UNROLL)]
        rh = [sb(f"rh{v}", [P, P], F32R) for v in range(4)]
        rl = [sb(f"rl{v}", [P, P], F32R) for v in range(4)]
        sgate = [sb(f"sgate{v}", [P, M]) for v in range(2)]
        hid = [sb(f"hid{v}", [P, M]) for v in range(2)]
        hidT = [sb(f"hidT{v}", [P, MC, P]) for v in range(2)]
        eo = [sb(f"eo{v}", [P, C]) for v in range(4)]
        late = gu_f[:].rearrange("p e m -> p (e m)")
        GC = G * C

        def late_view(at, n):
            return late[:, at * GC:(at + n) * GC]

        yin = [late_view(2 * u, 2).rearrange("p (k i c) -> p k i c", k=TOPK, i=G) for u in range(2)]
        z0 = [late_view(4 + u, 1).rearrange("p (i c) -> p i c", i=G) for u in range(2)]
        z1 = [late_view(6 + u, 1).rearrange("p (i c) -> p i c", i=G) for u in range(2)]
        fo = tln

        bank = [ctx.enter_context(nc.psum_tensor(f"bank{i}", [P, 512], F32)) for i in range(8)]
        xnT_ps = bank[0:2]
        S_ps = bank[2:4]
        prep_ps = bank[4]
        chain_ps = [bank[5 + b][:, 0:P] for b in range(B)]
        LT_ps = bank[7][:, 0:P]
        outT_ps, attn_ps, xtT_ps, small_ps = bank[0], bank[1], bank[2], bank[3]
        lg_ps = small_ps[:, 0:G * 2 * E].rearrange("p (i w e) -> p i w e", i=G, w=2)
        pre_ps = small_ps[:, 128:128 + (G + 1) * E].rearrange("p (i e) -> p i e", i=G + 1)
        rowT_ps = bank[0:2]
        gu_ps = bank[4:6]
        hidT_ps = {False: [bank[6][:, 0:M]] * 2, True: [bank[6][:, 0:M], bank[2][:, 0:M]]}
        y_ps = {False: [bank[7][:, 0:C]] * 2, True: [bank[7][:, 0:C], bank[3][:, 0:C]]}

        waits_apart = sem("waits_apart")
        x_in = [sem(f"x_in{q}") for q in range(QS)]
        attn_w_in = sem("attn_w_in")
        metric_in = sem("metric_in")
        router_w_in = sem("router_w_in")
        gu_in = sem("gu_in")
        down_in = sem("down_in")
        zeroed = sem("zeroed")
        consts = sem("consts")
        pool_chain = sem("pool_chain")
        prep_mm = sem("prep_mm")
        prep_sb = sem("prep_sb")
        metric_ready = sem("metric_ready")
        gw_lo_done = sem("gw_lo_done")
        gu_hi_done = sem("gu_hi_done")
        gu_lo_done = sem("gu_lo_done")
        st1_w = sem("st1_w")
        mv1_done = sem("mv1_done")
        ln1_c = sem("ln1_c")
        xn_done = sem("xn_done")
        gram_tr = sem("gram_tr")
        xnT_done = sem("xnT_done")
        chain_mm = sem("chain_mm")
        chain_sb = sem("chain_sb")
        gm_done = sem("gm_done")
        outT_mm = sem("outT_mm")
        outT_sb = sem("outT_sb")
        attn_tr = sem("attn_tr")
        st2_w = sem("st2_w")
        mv2_done = sem("mv2_done")
        ln2_c = sem("ln2_c")
        tln_done = sem("tln_done")
        x1_done = sem("x1_done")
        st3_w = sem("st3_w")
        mv3_done = sem("mv3_done")
        ln3_c = sem("ln3_c")
        xt_done = sem("xt_done")
        xtT_tr = sem("xtT_tr")
        xh_done = sem("xh_done")
        xl_done = sem("xl_done")
        logits_mm = sem("logits_mm")
        r1_c = sem("r1_c")
        R1 = 5
        mask_done = sem("mask_done")
        logits_sb = sem("logits_sb")
        th_done = sem("th_done")
        rb_c = sem("rb_c")
        RB = 3
        prefix_mm = sem("prefix_mm")
        r2_c = sem("r2_c")
        R2 = 4
        src_done = sem("src_done")
        rows_out = [sem(f"rows_out{u}") for u in range(2)]
        empty_out = sem("empty_out")
        pads_out = sem("pads_out")
        tab_c = sem("tab_c")
        pad_ready = sem("pad_ready")
        tables = sem("tables")
        gu_mm = sem("gu_mm")
        silu_done = sem("silu_done")
        hid_done = sem("hid_done")
        hidT_tr = sem("hidT_tr")
        hidT_done = sem("hidT_done")
        y_mm = sem("y_mm")
        ysh_done = sem("ysh_done")
        eo_done = sem("eo_done")
        row_in = [sem(f"row_in{v}") for v in range(UNROLL)]
        rowT_tr = sem("rowT_tr")
        rh_done = sem("rh_done")
        rl_done = sem("rl_done")
        res_out = [sem(f"res_out{v}") for v in range(4)]
        y_in = [sem(f"y_in{u}") for u in range(2)]
        z0_done = sem("z0_done")
        z1_done = sem("z1_done")
        st4_w = sem("st4_w")
        mv4_done = sem("mv4_done")
        ln4_c = sem("ln4_c")
        fo_done = sem("fo_done")
        sum_done = sem("sum_done")
        out_sent = [sem(f"out_sent{u}") for u in range(2)]

        block = ctx.enter_context(nc.Block())

        def after(eng, s, value):
            if not isinstance(value, int) or value > 0:
                eng.wait_ge(s, value)

        def wait_apart(eng, s, value):
            eng.wait_ge(s, value)
            if not isinstance(value, int):
                eng.sem_inc(waits_apart, 1)

        def back(q, u, d):
            v = (u - d) % 2
            return q - (d - u + v) // 2, v

        def num(q, u):
            return q * 2 + u

        def exists(q):
            return not isinstance(q, int) or 0 <= q < QS

        def steps(eng, body):
            for u in range(2):
                body(0, u)
            with eng.Fori(1, QS) as q:
                for u in range(2):
                    body(q, u)

        def steps_lagged(eng, body):
            steps(eng, body)
            body(QS, 0)

        def slots(eng, body, lag):
            for v in range(UNROLL):
                body(v, v)
            with eng.Fori(1, SLOTS // UNROLL - 1) as j:
                for v in range(UNROLL):
                    body(j * UNROLL + v, v)
            for v in range(UNROLL + lag):
                body(SLOTS - UNROLL + v, v % UNROLL)

        def tiles(t, q, u):
            return t[:, u, bass.ds(q * G, G)]

        def bc(ap, axis, shape):
            return ap.unsqueeze(axis).to_broadcast(shape)

        @block.sync
        def _(sp):
            for q in range(QS):
                for u in range(B):
                    sp.dma_start(X[:, u, q * G:(q + 1) * G, :],
                                 x_v[:, u, q * G:(q + 1) * G, :]).then_inc(x_in[q], 16)
            sp.dma_start(gu_f[:, E, 0:M], sg[0]).then_inc(gu_in, 16)
            sp.dma_start(gu_f[:, E, M:2 * M], su[0]).then_inc(gu_in, 16)
            sp.dma_start(gu_f[:, 0:E, 0:M], wg.rearrange("e h m -> h e m")).then_inc(gu_in, 16)
            sp.dma_start(gu_f[:, 0:E, M:2 * M], wu.rearrange("e h m -> h e m")).then_inc(gu_in, 16)
            sp.dma_start(down[:, E, :, :], sd[0].rearrange("(a p) h -> p a h", p=P)).then_inc(down_in, 16)
            for e in range(E):
                sp.dma_start(down[:, e, :, :],
                             wd[e].rearrange("(a p) h -> p a h", p=P)).then_inc(down_in, 16)

            sp.wait_ge(tables, 1)
            for u in range(2):
                sp.wait_ge(rows_out[u], 16 * G * TOPK * QS)
            sp.wait_ge(empty_out, 16)
            sp.wait_ge(pads_out, 16 * E)

            def load(r, v):
                after(sp, res_out[v % 4], (r - UNROLL + 4) * 4 - (v % 4) * 4)
                row = sp.value_load(row_i[0:1, bass.ds(r, 1)], min_val=0, max_val=EMPTY_REGION)
                sp.dma_start(rowt[v][:, :], rows_d[bass.ds(row, P), :]).then_inc(row_in[v], 16)

            for v in range(UNROLL):
                load(v, v)
            with sp.Fori(1, SLOTS // UNROLL) as j:
                for v in range(UNROLL):
                    load(j * UNROLL + v, v)

            for v in range(4):
                sp.wait_ge(res_out[v], 16 * SLOTS // 4)

            def results(q, u):
                after(sp, z1_done, num(q, u) - 1)
                for k in range(TOPK):
                    sp.dma_start(yin[u][:, k],
                                 res_v[:, k, bass.ds(q * G + u * TPB, G), :]).then_inc(y_in[u], 16)

            def output(q, u):
                sp.wait_ge(sum_done, num(q, u) + 1)
                sp.dma_start(tiles(out_v, q, u), fo[u][:]).then_inc(out_sent[u], 16)

            def last(q, u):
                q2, u2 = back(q, u, 2)
                if exists(q):
                    results(q, u)
                if exists(q2):
                    output(q2, u2)

            steps(sp, last)
            last(QS, 0)
            last(QS, 1)
            for u in range(2):
                sp.wait_ge(out_sent[u], 16 * QS)

        @block.gpsimd
        def _(gp):
            done = [0]

            def link(ins):
                done[0] += 1
                ins.then_inc(pool_chain, 1)
                gp.wait_ge(pool_chain, done[0])

            nc.gpsimd.memset(ucomp[:], 0.0).then_inc(zeroed, 1)
            nc.gpsimd.memset(mhalf[:], -0.5)
            link(nc.gpsimd.memset(ident[:], 0.0))
            link(nc.gpsimd.affine_select(out=ident[:], in_=ident[:], compare_op=ALU.not_equal, fill=1.0,
                                         base=0, pattern=[[-1, P]], channel_multiplier=1))
            link(nc.gpsimd.memset(headmask[:], 1.0))
            link(nc.gpsimd.affine_select(out=headmask[:], in_=headmask[:], compare_op=ALU.is_ge, fill=0.0,
                                         base=0, pattern=[[-K, H], [0, K]], channel_multiplier=1))
            link(nc.gpsimd.affine_select(out=headmask[:], in_=headmask[:], compare_op=ALU.is_ge, fill=0.0,
                                         base=K - 1, pattern=[[K, H], [0, K]], channel_multiplier=-1))
            nc.gpsimd.memset(ones_b[:], 1.0)
            link(nc.gpsimd.memset(below[:], 1.0))
            link(nc.gpsimd.affine_select(out=below[:], in_=below[:], compare_op=ALU.is_gt, fill=0.0,
                                         base=0, pattern=[[1, P]], channel_multiplier=-1))
            nc.gpsimd.memset(mask[:], 0.0)
            nc.gpsimd.iota(iota8[:], pattern=[[1, E]], base=0, channel_multiplier=0, allow_small_or_imprecise_dtypes=True)
            nc.gpsimd.iota(regbase[:], pattern=[[REGION, E]], base=0, channel_multiplier=0, allow_small_or_imprecise_dtypes=True)
            nc.gpsimd.iota(carry[:], pattern=[[REGION, E]], base=0, channel_multiplier=0, allow_small_or_imprecise_dtypes=True)
            nc.gpsimd.iota(pidx[:], pattern=[[0, 1]], base=0, channel_multiplier=1, allow_small_or_imprecise_dtypes=True)
            nc.gpsimd.iota(iota_t[:], pattern=[[1, SLOTS]], base=0, channel_multiplier=0, allow_small_or_imprecise_dtypes=True)
            nc.gpsimd.iota(ids[:], pattern=[[T, TOPK], [TPB, B], [1, TPB]], base=0,
                           channel_multiplier=TILES)
            for u in range(2):
                nc.gpsimd.memset(src[u][:], 0.0)
            link(nc.gpsimd.memset(upto[:], 1.0))
            link(nc.gpsimd.affine_select(out=upto[:], in_=upto[:], compare_op=ALU.is_ge, fill=0.0,
                                         base=0, pattern=[[1, E], [-1, E]], channel_multiplier=0))
            link(nc.gpsimd.memset(empty_row[:], 0.0))
            link(nc.gpsimd.memset(empty_row[:, P:P + 1].bitcast(I32), NOWHERE))
            nc.gpsimd.dma_start(rows_d[EMPTY_REGION:EMPTY_REGION + P, :], empty_row[:]).then_inc(empty_out, 16)
            gp.engine_nop().then_inc(consts, 1)

            gp.wait_ge(metric_in, 16 * K)
            nc.gpsimd.tensor_tensor(ubig[:].rearrange("p (h k) -> p h k", h=H),
                                    bc(ucomp[:], 1, [P, H, K]), headmask[:], ALU.mult)
            link(nc.gpsimd.tensor_scalar(iddiag[:], ident[:], dcomp[:], None, ALU.mult))
            nc.gpsimd.tensor_tensor(udiag[:], ubig[:], iddiag[:], ALU.add).then_inc(metric_ready, 1)

            def norm(mv_u, vpe_u, rstd_u, s, base):
                nc.gpsimd.tensor_scalar(vpe_u[:], mv_u[:, :, 1], EPS, None, ALU.add).then_inc(s, 1)
                gp.wait_ge(s, base + 1)
                nc.gpsimd.tensor_tensor(rstd_u[:], vpe_u[:], mhalf[:], ALU.pow).then_inc(s, 1)

            def norm_shift(mv_u, vpe_u, rstd_u, nmean_u, shift_u, s, base):
                nc.gpsimd.tensor_scalar(nmean_u[:], mv_u[:, :, 0], -1.0, None, ALU.mult).then_inc(s, 1)
                norm(mv_u, vpe_u, rstd_u, s, base + 1)
                gp.wait_ge(s, base + 3)
                nc.gpsimd.tensor_tensor(shift_u[:], nmean_u[:], rstd_u[:], ALU.mult).then_inc(s, 1)

            def ln1(q, u):
                after(gp, xn_done, num(q, u) - 1)
                wait_apart(gp, mv1_done, num(q, u) + 1)
                norm_shift(mv[u], vpe[u], rstd[u], nmean[u], shift[u], ln1_c, num(q, u) * 4)

            steps(gp, ln1)

            gp.wait_ge(prep_sb, 2)
            nc.gpsimd.tensor_tensor(gw2[:, 1, :], gwT[:], gw2[:, 0, :].bitcast(F32),
                                    ALU.subtract).then_inc(gw_lo_done, 1)
            for n, e in enumerate([E, *range(E)]):
                gp.wait_ge(gu_hi_done, n + 1)
                nc.gpsimd.tensor_tensor(gu_lo[:, e, :], gu_f[:, e, :], gu_hi[:, e, :].bitcast(F32),
                                        ALU.subtract).then_inc(gu_lo_done, 1)

            def scatter(q, u, tiles_of):
                wait_apart(gp, src_done, num(q, u) + 1)
                for i in tiles_of:
                    for k in range(TOPK):
                        nc.gpsimd.indirect_dma_start(
                            rows_d, bass.IndirectOffsetOnAxis(ap=slot[u][:, i, k:k + 1], axis=0),
                            src[u][:, k, i, :], None).then_inc(rows_out[u], 16)

            def attn_step(q, u):
                q1, u1 = back(q, u, 1)
                q2, u2 = back(q, u, 2)
                if exists(q):
                    wait_apart(gp, mv2_done, num(q, u) + 1)
                    norm_shift(mv[u], vpe[u], rstd[u], nmean[u], shift[u], ln2_c, num(q, u) * 4)
                if exists(q2):
                    scatter(q2, u2, range(2, G))
                if exists(q):
                    wait_apart(gp, mv3_done, num(q, u) + 1)
                    norm(mv3[u], vpe3[u], rstd3[u], ln3_c, num(q, u) * 2)
                if exists(q1):
                    scatter(q1, u1, range(0, 2))

            steps(gp, attn_step)
            attn_step(QS, 0)
            attn_step(QS, 1)
            gp.wait_ge(pad_ready, 1)
            for e in range(E):
                nc.gpsimd.indirect_dma_start(
                    rows_d, bass.IndirectOffsetOnAxis(ap=padidx[:, e:e + 1], axis=0),
                    empty_row[:], None).then_inc(pads_out, 16)

            def store(r, v):
                wait_apart(gp, eo_done, r + 1)
                nc.gpsimd.indirect_dma_start(
                    res_d, bass.IndirectOffsetOnAxis(ap=rowt[v][:, P:P + 1].bitcast(U32), axis=0),
                    eo[v % 4][:], None, bounds_check=TOPK * T - 1, oob_is_err=False
                ).then_inc(res_out[v % 4], 16)

            slots(gp, store, 0)

            def last(q, u):
                q1, u1 = back(q, u, 1)
                if exists(q):
                    wait_apart(gp, mv4_done, num(q, u) + 1)
                    norm_shift(mv[u], vpe[u], rstd[u], nmean[u], shift[u], ln4_c, num(q, u) * 4)
                if exists(q1):
                    gp.wait_ge(fo_done, num(q1, u1) + 1)
                    nc.gpsimd.tensor_tensor(fo[u1][:], fo[u1][:], tiles(x1, q1, u1), ALU.add).then_inc(sum_done, 1)

            steps_lagged(gp, last)

        def silu(act, g, v):
            act.wait_ge(gu_mm, g + 1)
            after(act, hid_done, g - 1)
            nc.scalar.activation(sgate[v][:], gu_ps[v][:, 0:M], ACT.Silu).then_inc(silu_done, 1)

        def hidT_copy(act, g, v, own=False):
            if isinstance(g, int) and g < 0:
                return
            act.wait_ge(hidT_tr, g + 1)
            after(act, y_mm, g - 1)
            nc.scalar.activation(hidT[v][:].rearrange("p a t -> p (a t)"), hidT_ps[own][v],
                                 ACT.Copy).then_inc(hidT_done, 1)

        @block.scalar
        def _(act):
            act.dma_start(Wc[:], proj[0].rearrange("n c k -> c n k")).then_inc(attn_w_in, 16)
            act.dma_start(mix[:], mixer_w).then_inc(attn_w_in, 16)
            act.dma_start(mixb[:], mixer_b.rearrange("(c a) -> c a", a=1), allow_slow_non_contiguous=True).then_inc(attn_w_in, 16)
            act.dma_start(gw[:], gate_w).then_inc(router_w_in, 16)
            act.dma_start(beta_sb[:], beta.partition_broadcast(P)).then_inc(router_w_in, 16)
            act.wait_ge(zeroed, 1)
            act.dma_start(dcomp[:], diag.rearrange("h (k a) -> (h k) a", a=1), allow_slow_non_contiguous=True).then_inc(metric_in, 16)
            off = 0
            for k in range(K - 1):
                act.dma_start(ucomp[k:P:K, k + 1:K], halves[:, off:off + K - 1 - k],
                              allow_slow_non_contiguous=True).then_inc(metric_in, 16)
                off += K - 1 - k

            act.wait_ge(prep_mm, 1)
            nc.scalar.activation(WT[:], prep_ps[:, 0:128], ACT.Copy)
            nc.scalar.activation(mixT[:], prep_ps[:, 128:256], ACT.Copy)
            nc.scalar.activation(gwT[:], prep_ps[:, 256:256 + E], ACT.Copy).then_inc(prep_sb, 1)
            act.wait_ge(prep_sb, 1)
            nc.scalar.activation(gw2[:, 0, :], gwT[:], ACT.Copy).then_inc(prep_sb, 1)
            def first(q, u):
                act.wait_ge(ln1_c, num(q, u) * 4 + 4)
                after(act, gram_tr, num(q, u) - 1)
                for i in range(G):
                    last = nc.scalar.activation(xn[u][:, i, :], X[:, u, bass.ds(q * G + i, 1), :].rearrange("p a c -> p (a c)"),
                                                ACT.Identity, bias=shift[u][:, i:i + 1], scale=rstd[u][:, i:i + 1])
                last.then_inc(xn_done, 1)

            steps(act, first)

            act.wait_ge(gram_tr, STEPS)
            for b in range(B):
                nc.scalar.activation(S_sb[b][:], S_ps[b][:, 0:P], ACT.Copy).then_inc(chain_sb, 1)
            act.wait_ge(prep_mm, 2)
            nc.scalar.activation(LT[:], LT_ps, ACT.Copy).then_inc(prep_sb, 1)
            for n, dst in ((0, T1), (2, R_sb), (3, A_sb)):
                for b in range(B):
                    act.wait_ge(chain_mm, n * B + b + 1)
                    nc.scalar.activation(dst[b][:], chain_ps[b], ACT.Copy).then_inc(chain_sb, 1)

            act.wait_ge(gu_in, 64)
            for e in (E, *range(E)):
                nc.scalar.activation(gu_hi[:, e, :], gu_f[:, e, :], ACT.Copy).then_inc(gu_hi_done, 1)

            def unit(q, u, i):
                g = num(q, u) * G + i
                silu(act, g, i % 2)
                hidT_copy(act, g - 1, (i - 1) % 2)
                ysh_copy(q, u, i - 2)

            def ysh_copy(q, u, i):
                if i < 0:
                    q, u = back(q, u, 1)
                    i += G
                    if not exists(q):
                        return
                g = num(q, u) * G + i
                act.wait_ge(y_mm, g + 1)
                nc.scalar.activation(ysh[:, u, bass.ds(q * G + i, 1), :].rearrange("p a c -> p (a c)"),
                                     y_ps[False][i % 2], ACT.Copy).then_inc(ysh_done, 1)

            def attn_step(q, u):
                q1, u1 = back(q, u, 1)
                if exists(q1):
                    s = num(q1, u1)
                    act.wait_ge(xtT_tr, s + 1)
                    after(act, gu_mm, (s - 1) * G)
                    nc.scalar.activation(xh[u1][:].rearrange("p i t -> p (i t)"), xtT_ps[:, :],
                                         ACT.Copy).then_inc(xh_done, 1)
                if exists(q):
                    s = num(q, u)
                    act.wait_ge(outT_mm, s + 1)
                    after(act, attn_tr, s - 1)
                    nc.scalar.activation(outT[u][:], outT_ps[:, :], ACT.Identity, bias=mixb[:]).then_inc(outT_sb, 1)
                if exists(q1):
                    unit(q1, u1, 0)
                    act.wait_ge(logits_sb, num(q1, u1) + 1)
                    after(act, rb_c, num(q1, u1) * RB)
                    nc.scalar.activation(th[:], logits[:], ACT.Tanh, scale=0.5).then_inc(th_done, 1)
                if exists(q):
                    s = num(q, u)
                    act.wait_ge(ln2_c, s * 4 + 4)
                    after(act, x1_done, s - 1)
                    for i in range(G):
                        last = nc.scalar.activation(tln[u][:, i, :], attn_ps[:, i * P:(i + 1) * P], ACT.Identity,
                                                    bias=shift[u][:, i:i + 1], scale=rstd[u][:, i:i + 1])
                    last.then_inc(tln_done, 1)
                if exists(q1):
                    for i in range(1, G):
                        unit(q1, u1, i)

            steps_lagged(act, attn_step)
            hidT_copy(act, TILES - 1, 1)
            ysh_copy(QS - 1, 1, 2)
            ysh_copy(QS - 1, 1, 3)

            def row_high(r, v):
                act.wait_ge(rowT_tr, r + 1)
                after(act, gu_mm, r - 4 + TILES + 1 if not isinstance(r, int) or r >= 4 else 0)
                nc.scalar.activation(rh[v % 4][:], rowT_ps[v % 2][:, 0:P], ACT.Copy).then_inc(rh_done, 1)

            def routed(r, v):
                if not isinstance(r, int) or r < SLOTS:
                    silu(act, r + TILES, v % 2)
                if not isinstance(r, int) or r + 2 < SLOTS:
                    row_high(r + 2, (v + 2) % UNROLL)
                if not isinstance(r, int) or 1 <= r <= SLOTS:
                    hidT_copy(act, r - 1 + TILES, (v - 1) % 2, True)

            row_high(0, 0)
            row_high(1, 1)
            slots(act, routed, 1)

            def last_step(q, u):
                s = num(q, u)
                act.wait_ge(ln4_c, s * 4 + 4)
                after(act, out_sent[u], q * 16)
                for i in range(G):
                    last = nc.scalar.activation(fo[u][:, i, :], z1[u][:, i, :], ACT.Identity,
                                                bias=shift[u][:, i:i + 1], scale=rstd[u][:, i:i + 1])
                last.then_inc(fo_done, 1)

            steps(act, last_step)

        @block.vector
        def _(dve):
            dve.wait_ge(consts, 1)

            def stats(src_of, st_u, mv_u, st_sem, mv_sem, s):
                for i in range(G):
                    last = nc.vector.bn_stats(st_u[:, i, :], src_of(i))
                last.then_inc(st_sem, 1)
                wait_apart(dve, st_sem, s + 1)
                for i in range(G):
                    last = nc.vector.bn_aggr(mv_u[:, i, :], st_u[:, i, :])
                last.then_inc(mv_sem, 1)

            def xnT_copy(q, u):
                s = num(q, u)
                dve.wait_ge(gram_tr, s + 1)
                nc.vector.tensor_copy(xnT[:, u, bass.ds(q * G * P, G * P)], xnT_ps[u][:, :]).then_inc(xnT_done, 1)

            def make_metric():
                dve.wait_ge(metric_ready, 1)
                dve.wait_ge(prep_sb, 1)
                nc.vector.tensor_tensor(metric[:], prep_ps[:, 384:512], udiag[:], ALU.add).then_inc(metric_ready, 1)

            for q in range(QS):
                dve.wait_ge(x_in[q], 32)
                for u in range(2):
                    s = num(q, u)
                    after(dve, ln1_c, (s - 1) * 4)
                    stats(lambda i: X[:, u, q * G + i, :], st[u], mv[u], st1_w, mv1_done, s)
                if q == 1:
                    make_metric()
                if q >= 1:
                    for u in range(2):
                        xnT_copy(q - 1, u)
            for u in range(2):
                xnT_copy(QS - 1, u)
            for b in range(B):
                dve.wait_ge(chain_mm, B + b + 1)
                nc.vector.tensor_tensor(Gm[b][:], chain_ps[b], headmask[:].rearrange("p h k -> p (h k)"), ALU.mult).then_inc(gm_done, 1)

            def hidden(g, v):
                dve.wait_ge(silu_done, g + 1)
                after(dve, hidT_tr, g - 1)
                nc.vector.tensor_tensor(hid[v][:], sgate[v][:], gu_ps[v][:, M:2 * M], ALU.mult).then_inc(hid_done, 1)

            def normalise(q, u):
                s = num(q, u)
                dve.wait_ge(ln3_c, s * 2 + 2)
                for i in range(G):
                    last = nc.vector.tensor_scalar(xt[u][:, i, :], x1[:, u, bass.ds(q * G + i, 1), :].rearrange("p a c -> p (a c)"),
                                                   mv3[u][:, i, 0:1], rstd3[u][:, i:i + 1], ALU.subtract, ALU.mult)
                last.then_inc(xt_done, 1)
                dve.wait_ge(xh_done, s + 1)
                nc.vector.tensor_tensor(xl[u][:].rearrange("p i t -> p (i t)"), xtT_ps[:, :],
                                        xh[u][:].rearrange("p i t -> p (i t)").bitcast(F32),
                                        ALU.subtract).then_inc(xl_done, 1)

            def choose(q, u):
                s = num(q, u)
                n = [0]

                def link(ins):
                    n[0] += 1
                    ins.then_inc(r1_c, 1)
                    wait_apart(dve, r1_c, s * R1 + n[0])

                dve.wait_ge(logits_mm, s + 1)
                after(dve, th_done, s)
                nc.vector.tensor_reduce(logits[:], lg_ps.rearrange("p i w e -> p i e w"), axis=AX.X,
                                        op=ALU.add).then_inc(logits_sb, 1)
                dve.wait_ge(logits_sb, s + 1)
                link(nc.vector.tensor_tensor(sel[:], logits[:], bc(beta_sb[:], 1, [P, G, E]), ALU.add))
                for i in range(G):
                    last = nc.vector.max(mx[:, i, :], sel[:, i, :])
                link(last)
                for i in range(G):
                    last = nc.vector.max_index(ix[:, i, :], mx[:, i, :], sel[:, i, :])
                link(last)
                link(nc.vector.tensor_copy(ixf[:], ix[:, :, 0:TOPK]))
                for i in range(G):
                    last = nc.vector.tensor_tensor(chosen[:, i], bc(iota8[:], 1, [P, TOPK, E]),
                                                   bc(ixf[:, i, :], 2, [P, TOPK, E]), ALU.is_equal)
                link(last)
                assert n[0] == R1
                after(dve, prefix_mm, s)
                nc.vector.tensor_tensor(mask[:, 0:G, :], chosen[:, :, 0, :], chosen[:, :, 1, :],
                                        ALU.add).then_inc(mask_done, 1)

            def pick(dst, values, s_link, base):
                for k in range(TOPK):
                    last = nc.vector.tensor_tensor(picked[:, :, k, :], chosen[:, :, k, :], values[:], ALU.mult)
                last.then_inc(s_link, 1)
                dve.wait_ge(s_link, base + 1)
                return nc.vector.tensor_reduce(dst, picked[:], axis=AX.X, op=ALU.add)

            def probabilities(q, u):
                s = num(q, u)
                dve.wait_ge(th_done, s + 1)
                nc.vector.tensor_scalar(sig[:], th[:], 0.5, 0.5, ALU.mult, ALU.add).then_inc(rb_c, 1)
                dve.wait_ge(rb_c, s * RB + 1)
                pick(tiles(ck, q, u), sig, rb_c, s * RB + 1).then_inc(rb_c, 1)

            def places(q, u):
                s = num(q, u)
                dve.wait_ge(prefix_mm, s + 1)
                dve.wait_ge(rb_c, s * RB + RB)
                nc.vector.tensor_tensor(place[:], pre_ps[:, 0:G, :], bc(carry[:], 1, [P, G, E]),
                                        ALU.add).then_inc(r2_c, 1)
                dve.wait_ge(r2_c, s * R2 + 1)
                pick(slotf[:], place, r2_c, s * R2 + 1).then_inc(r2_c, 1)
                nc.vector.tensor_tensor(carry[:], carry[:], pre_ps[:, G, :], ALU.add).then_inc(r2_c, 1)
                dve.wait_ge(r2_c, s * R2 + R2)
                after(dve, rows_out[u], q * 16 * G * TOPK)
                nc.vector.tensor_copy(slot[u][:], slotf[:])
                for k in range(TOPK):
                    nc.vector.tensor_copy(src[u][:, k, :, 0:P], xt[u][:])
                    last = nc.vector.tensor_copy(src[u][:, k, :, P:P + 1].bitcast(I32),
                                                 ids[:, k, u, bass.ds(q * G, G)].unsqueeze(2))
                last.then_inc(src_done, 1)

            def attn_step(q, u):
                q1, u1 = back(q, u, 1)
                if exists(q1):
                    g1 = num(q1, u1) * G
                    normalise(q1, u1)
                    choose(q1, u1)
                    hidden(g1, 0)
                if exists(q):
                    s = num(q, u)
                    dve.wait_ge(attn_tr, s + 1)
                    after(dve, tln_done, s - 1)
                    stats(lambda i: attn_ps[:, i * P:(i + 1) * P], st[u], mv[u], st2_w, mv2_done, s)
                if exists(q1):
                    probabilities(q1, u1)
                    hidden(g1 + 1, 1)
                if exists(q):
                    dve.wait_ge(tln_done, s + 1)
                    nc.vector.tensor_tensor(tiles(x1, q, u), tln[u][:], tiles(X, q, u), ALU.add).then_inc(x1_done, 1)
                    wait_apart(dve, x1_done, s + 1)
                    stats(lambda i: x1[:, u, bass.ds(q * G + i, 1), :].rearrange("p a c -> p (a c)"),
                          st3[u], mv3[u], st3_w, mv3_done, s)
                if exists(q1):
                    places(q1, u1)
                    hidden(g1 + 2, 0)
                    hidden(g1 + 3, 1)

            steps_lagged(dve, attn_step)

            n = [0]

            def link(ins):
                n[0] += 1
                ins.then_inc(tab_c, 1)
                dve.wait_ge(tab_c, n[0])

            link(nc.vector.tensor_tensor(padidx_f[:], carry[:], pidx[:].to_broadcast([P, E]), ALU.add))
            nc.vector.tensor_copy(padidx[:], padidx_f[:]).then_inc(pad_ready, 1)
            link(nc.vector.tensor_tensor(cnt[:], carry[0:1, :], regbase[0:1, :], ALU.subtract))
            link(nc.vector.tensor_scalar(cnti[:], cnt[:], float(P - 1), None, ALU.add))
            link(nc.vector.tensor_scalar(ntiles_i[:], cnti[:], 7, None, ALU.logical_shift_right))
            link(nc.vector.tensor_copy(ntiles[:], ntiles_i[:]))
            nc.vector.tensor_scalar(step_of[:], ntiles[:], float(-P), float(REGION), ALU.mult, ALU.add)
            link(nc.vector.tensor_tensor(ends8[:], upto[:], bc(ntiles[:], 1, [1, E, E]), ALU.mult))
            link(nc.vector.tensor_reduce(ends[:], ends8[:], axis=AX.X, op=ALU.add))
            link(nc.vector.tensor_tensor(past[:], bc(iota_t[:], 2, [1, SLOTS, E]), bc(ends[:], 1, [1, SLOTS, E]),
                                         ALU.is_ge))
            nc.vector.tensor_tensor(past_s[:], past[:], bc(step_of[:], 1, [1, SLOTS, E]), ALU.mult)
            link(nc.vector.tensor_reduce(exp_f[:], past[:], axis=AX.X, op=ALU.add))
            nc.vector.tensor_scalar(exp_i[:], exp_f[:], float(E - 1), None, ALU.min)
            link(nc.vector.tensor_reduce(row_f[:], past_s[:], axis=AX.X, op=ALU.add))
            link(nc.vector.scalar_tensor_tensor(out=row_g[:], in0=iota_t[:], scalar=float(P), in1=row_f[:],
                                                op0=ALU.mult, op1=ALU.add))
            nc.vector.tensor_scalar(row_i[:], row_g[:], float(EMPTY_REGION), None, ALU.min).then_inc(tables, 1)

            def row_low(r, v):
                dve.wait_ge(rh_done, r + 1)
                nc.vector.tensor_tensor(rl[v % 4][:], rowT_ps[v % 2][:, 0:P], rh[v % 4][:].bitcast(F32),
                                        ALU.subtract).then_inc(rl_done, 1)

            def routed(r, v):
                if not isinstance(r, int) or r < SLOTS:
                    hidden(r + TILES, v % 2)
                if not isinstance(r, int) or r + 2 < SLOTS:
                    row_low(r + 2, (v + 2) % UNROLL)
                if not isinstance(r, int) or r >= 2:
                    w = (v - 2) % UNROLL
                    dve.wait_ge(y_mm, r - 2 + TILES + 1)
                    after(dve, res_out[w % 4], (r - 2 - w % 4) * 4)
                    nc.vector.tensor_copy(eo[w % 4][:], y_ps[True][w % 2]).then_inc(eo_done, 1)

            row_low(0, 0)
            row_low(1, 1)
            slots(dve, routed, 2)

            def last_step(q, u):
                s = num(q, u)
                dve.wait_ge(y_in[u], q * 32 + 32)
                if isinstance(q, int) and s == 0:
                    dve.wait_ge(ysh_done, TILES)
                for i in range(G):
                    last = nc.vector.scalar_tensor_tensor(
                        out=z0[u][:, i, :], in0=yin[u][:, 0, i, :],
                        scalar=ck[:, u, bass.ds(q * G + i, 1), 0:1].rearrange("p a k -> p (a k)"),
                        in1=ysh[:, u, bass.ds(q * G + i, 1), :].rearrange("p a c -> p (a c)"), op0=ALU.mult, op1=ALU.add)
                last.then_inc(z0_done, 1)
                dve.wait_ge(z0_done, s + 1)
                after(dve, fo_done, s - 1)
                for i in range(G):
                    last = nc.vector.scalar_tensor_tensor(
                        out=z1[u][:, i, :], in0=yin[u][:, 1, i, :],
                        scalar=ck[:, u, bass.ds(q * G + i, 1), 1:2].rearrange("p a k -> p (a k)"),
                        in1=z0[u][:, i, :], op0=ALU.mult, op1=ALU.add)
                last.then_inc(z1_done, 1)
                dve.wait_ge(z1_done, s + 1)
                after(dve, ln4_c, (s - 1) * 4)
                stats(lambda i: z1[u][:, i, :], st[u], mv[u], st4_w, mv4_done, s)

            steps(dve, last_step)

        @block.tensor
        def _(pe):
            mm = nc.tensor.matmul
            pe.wait_ge(consts, 1)
            pe.wait_ge(attn_w_in, 48)
            pe.wait_ge(router_w_in, 32)
            pe.wait_ge(metric_ready, 1)
            nc.tensor.transpose(prep_ps[:, 0:128], Wc[:].rearrange("p h k -> p (h k)"), ident[:])
            nc.tensor.transpose(prep_ps[:, 128:256], mix[:], ident[:])
            nc.tensor.transpose(prep_ps[:, 256:256 + E], gw[:], ident[0:E, 0:E])
            nc.tensor.transpose(prep_ps[:, 384:512], ubig[:], ident[:]).then_inc(prep_mm, 1)

            def first(q, u):
                s = num(q, u)
                pe.wait_ge(xn_done, s + 1)
                after(pe, xnT_done, s - 1)
                for i in range(G):
                    mm(S_ps[u][:, 0:P], xn[u][:, i, :], xn[u][:, i, :], start=isinstance(q, int) and i == 0,
                       stop=i == G - 1, skip_group_check=True)
                for i in range(G):
                    last = nc.tensor.transpose(xnT_ps[u][:, i * P:(i + 1) * P], xn[u][:, i, :], ident[:])
                last.then_inc(gram_tr, 1)

            steps(pe, first)

            pe.wait_ge(metric_ready, 2)
            pe.wait_ge(prep_sb, 1)
            mm(LT_ps, metric[:], WT[:], start=True, stop=True).then_inc(prep_mm, 1)
            pe.wait_ge(prep_sb, 3)

            Wf = Wc[:].rearrange("p h k -> p (h k)")
            for lhs, rhs, ready, at in ((S_sb, None, chain_sb, 0), (None, T1, chain_sb, B),
                                        (Gm, mixT, gm_done, 0), (LT, R_sb, chain_sb, 2 * B)):
                for b in range(B):
                    pe.wait_ge(ready, at + b + 1)
                    left = Wf if lhs is None else lhs[:] if lhs is LT else lhs[b][:]
                    right = Wf if rhs is None else rhs[:] if rhs is mixT else rhs[b][:]
                    mm(chain_ps[b], left, right, start=True, stop=True).then_inc(chain_mm, 1)
            pe.wait_ge(chain_sb, 4 * B)
            pe.wait_ge(xnT_done, STEPS)

            def gate_up(g, v, hi, lo, e):
                after(pe, hid_done, g - 1)
                mm(gu_ps[v][:, :], hi, gu_hi[:, e, :], start=True, stop=False)
                mm(gu_ps[v][:, :], hi, gu_lo[:, e, :], start=False, stop=False)
                mm(gu_ps[v][:, :], lo, gu_hi[:, e, :], start=False, stop=True).then_inc(gu_mm, 1)

            def hidden_T(g, v, own=False):
                if isinstance(g, int) and g < 0:
                    return
                pe.wait_ge(hid_done, g + 1)
                after(pe, hidT_done, g - 1 if own else g)
                for a in range(MC):
                    last = nc.tensor.transpose(hidT_ps[own][v][:, a * P:(a + 1) * P], hid[v][:, a * P:(a + 1) * P], ident[:])
                last.then_inc(hidT_tr, 1)

            def result(g, v, e, own=False):
                pe.wait_ge(hidT_done, g + 1)
                for a in range(MC):
                    last = mm(y_ps[own][v], hidT[v][:, a, :], down[:, e, a, :], start=a == 0, stop=a == MC - 1)
                last.then_inc(y_mm, 1)

            def shared(q, u, i):
                g = num(q, u) * G + i
                gate_up(g, i % 2, xh[u][:, i, :], xl[u][:, i, :], E)
                hidden_T(g - 1, (i - 1) % 2)
                if not isinstance(g, int) or g >= 2:
                    after(pe, ysh_done, g - 2)
                    result(g - 2, i % 2, E)

            def attn_step(q, u):
                q1, u1 = back(q, u, 1)
                s = num(q, u)
                s1 = num(q1, u1)
                if exists(q1):
                    pe.wait_ge(xt_done, s1 + 1)
                    after(pe, xl_done, s1)
                    for i in range(G):
                        last = nc.tensor.transpose(xtT_ps[:, i * P:(i + 1) * P], xt[u1][:, i, :], ident[:])
                    last.then_inc(xtT_tr, 1)
                if exists(q):
                    after(pe, outT_sb, s)
                    mm(outT_ps[:, :], A_sb[u][:], xnT[:, u, bass.ds(q * G * P, G * P)], start=True,
                       stop=True).then_inc(outT_mm, 1)
                if exists(q1):
                    pe.wait_ge(xl_done, s1 + 1)
                    if isinstance(s1, int) and s1 == 0:
                        pe.wait_ge(gw_lo_done, 1)
                        pe.wait_ge(gu_lo_done, 1)
                        pe.wait_ge(down_in, 16 * (E + 1))
                    after(pe, r1_c, s1 * R1)
                    after(pe, r2_c, s1 * R2)
                    for i in range(G):
                        for n, part in enumerate((xh, xl)):
                            last = mm(lg_ps[:, i].rearrange("p w e -> p (w e)"), part[u1][:, i, :],
                                      gw2[:].rearrange("p w e -> p (w e)"), start=n == 0, stop=n == 1)
                    last.then_inc(logits_mm, 1)
                    shared(q1, u1, 0)
                if exists(q):
                    pe.wait_ge(outT_sb, s + 1)
                    after(pe, tln_done, s)
                    for i in range(G):
                        last = nc.tensor.transpose(attn_ps[:, i * P:(i + 1) * P], outT[u][:, i * P:(i + 1) * P], ident[:])
                    last.then_inc(attn_tr, 1)
                if exists(q1):
                    shared(q1, u1, 1)
                    pe.wait_ge(mask_done, s1 + 1)
                    mm(pre_ps, below[:], mask[:], start=True, stop=False)
                    for i in range(G):
                        last = mm(pre_ps[:, i + 1:G + 1, :], ones_b[:], bc(mask[:, i, :], 1, [P, G - i, E]),
                                  start=False, stop=i == G - 1)
                    last.then_inc(prefix_mm, 1)
                    shared(q1, u1, 2)
                    shared(q1, u1, 3)

            steps_lagged(pe, attn_step)
            hidden_T(TILES - 1, 1)
            pe.wait_ge(ysh_done, TILES - 2)
            result(TILES - 2, 0, E)
            pe.wait_ge(ysh_done, TILES - 1)
            result(TILES - 1, 1, E)
            pe.wait_ge(ysh_done, TILES)

            pe.wait_ge(tables, 1)
            pe.wait_ge(gu_lo_done, E + 1)

            def row_T(r, v):
                pe.wait_ge(row_in[v], (r - v) * 2 + 16)
                after(pe, rl_done, r - 1)
                nc.tensor.transpose(rowT_ps[v % 2][:, 0:P], rowt[v][:, 0:P], ident[:]).then_inc(rowT_tr, 1)

            experts = {}

            def routed(r, v):
                if not isinstance(r, int) or r < SLOTS:
                    e = pe.value_load(exp_i[0:1, bass.ds(r, 1)], min_val=0, max_val=E - 1)
                    pe.wait_ge(rl_done, r + 1)
                    gate_up(r + TILES, v % 2, rh[v % 4][:], rl[v % 4][:], bass.ds(e, 1))
                if not isinstance(r, int) or r + 2 < SLOTS:
                    row_T(r + 2, (v + 2) % UNROLL)
                if not isinstance(r, int) or 1 <= r <= SLOTS:
                    hidden_T(r - 1 + TILES, (v - 1) % 2, True)
                if not isinstance(r, int) or r >= 2:
                    e = pe.value_load(exp_i[0:1, bass.ds(r - 2, 1)], min_val=0, max_val=E - 1)
                    after(pe, eo_done, r - 3)
                    result(r - 2 + TILES, v % 2, bass.ds(e, 1), True)

            row_T(0, 0)
            row_T(1, 1)
            slots(pe, routed, 2)


_INS = ["L0_attn_in_sequence_bwc", "L0_attn_projection_1nck", "L0_attn_halves", "L0_attn_diagonals_nk",
        "L0_attn_mixer_w", "L0_attn_mixer_b", "L0_ffn_gate_w", "L0_ffn_beta", "L0_ffn_gate_proj_w",
        "L0_ffn_up_proj_w", "L0_ffn_down_proj_w", "L0_ffn_shared_gate_w", "L0_ffn_shared_up_w",
        "L0_ffn_shared_down_w"]


def kernel(**inputs):
    import numpy as np
    import concourse.bacc as bacc
    from concourse.bass_utils import run_bass_kernel_spmd

    nc = bacc.Bacc("TRN2", target_bir_lowering=False, num_devices=1)
    arrays, args = {}, []
    for name in _INS:
        a = np.ascontiguousarray(inputs[name])
        arrays[f"in_{name}"] = a
        args.append(nc.dram_tensor(f"in_{name}", a.shape, mybir.dt.from_np(a.dtype), kind="ExternalInput").ap())
    shape = inputs[_INS[0]].shape
    args.append(nc.dram_tensor("out_0", shape, F32, kind="ExternalOutput").ap())
    build_sandwich(nc, *args)
    r = run_bass_kernel_spmd(nc, [arrays], core_ids=[0])
    return r.results[0]["out_0"]
```

```python
from contextlib import ExitStack

import concourse.bass as bass
from concourse import mybir

F32 = mybir.dt.float32
F32R = mybir.dt.float32r
BF16 = mybir.dt.bfloat16
I32 = mybir.dt.int32
U32 = mybir.dt.uint32
ALU = mybir.AluOpType
ACT = mybir.ActivationFunctionType
AX = mybir.AxisListType

P = 128
G = 4
EPS = 1e-5
TOPK = 2


def build_sandwich(nc, x, proj, halves, diag, mixer_w, mixer_b, gate_w, beta,
                   wg, wu, wd, sg, su, sd, out):
    B, W, C = x.shape
    H, K = diag.shape
    E, _, M = wg.shape
    MC = M // P
    TPB = W // P
    TILES = B * TPB
    QS = TPB // G
    STEPS = B * QS
    T = B * W
    assert C == P and H * K == P and B == 2 and TOPK * M == 4 * P

    REGION = T + P
    ROW = P + 4
    EMPTY_REGION = E * REGION
    UNROLL = 8
    SLOTS = -(-((TOPK * T + E * (P - 1)) // P) // UNROLL) * UNROLL
    NOWHERE = TOPK * T

    x_v = x.rearrange("b (p j) c -> p b j c", p=P)
    out_v = out.rearrange("b (p j) c -> p b j c", p=P)

    with ExitStack() as ctx:
        def sb(name, shape, dt=F32):
            return ctx.enter_context(nc.sbuf_tensor(name, shape, dt))

        def sem(name):
            return ctx.enter_context(nc.semaphore(name))

        rows_d = nc.dram_tensor("expert_rows", [EMPTY_REGION + P, ROW], F32).ap()
        res_d = nc.dram_tensor("expert_results", [TOPK * T, C], F32).ap()
        res_v = res_d.rearrange("(k p t) c -> p k t c", k=TOPK, p=P)

        X = sb("X", [P, B, TPB, C])
        xnT = sb("xnT", [P, B, TPB * P])
        x1 = sb("x1", [P, B, TPB, C])
        ysh = sb("ysh", [P, B, TPB, C])
        ids = sb("ids", [P, TOPK, B, TPB], I32)
        gu_f = sb("gu_f", [P, E + 1, 2 * M])
        gu_hi = sb("gu_hi", [P, E + 1, 2 * M], F32R)
        gu_lo = sb("gu_lo", [P, E + 1, 2 * M], F32R)
        down = sb("down", [P, E + 1, MC, C])
        ident = sb("ident", [P, P])
        headmask = sb("headmask", [P, H, K])
        below = sb("below", [P, P], BF16)
        ones_b = sb("ones_b", [P, P], BF16)
        iota8 = sb("iota8", [P, E])
        centre = sb("centre", [P, P])
        ones_row = sb("ones_row", [1, P])
        iota_t = sb("iota_t", [1, SLOTS])
        upto = sb("upto", [1, E, E])
        regbase = sb("regbase", [P, E])
        mhalf = sb("mhalf", [P, G])
        pidx = sb("pidx", [P, 1])
        empty_row = sb("empty_row", [P, ROW])
        Wc = sb("Wc", [P, H, K])
        WT = sb("WT", [P, P])
        mix = sb("mix", [P, C])
        mixT = sb("mixT", [P, C])
        mixb = sb("mixb", [P, 1])
        mixb_c = sb("mixb_c", [P, 1])
        ucomp = sb("ucomp", [P, K])
        dcomp = sb("dcomp", [P, 1])
        ubig = sb("ubig", [P, P])
        udiag = sb("udiag", [P, P])
        iddiag = sb("iddiag", [P, P])
        metric = sb("metric", [P, P])
        LT = sb("LT", [P, P])
        gw = sb("gw", [E, C])
        gwT = sb("gwT", [P, E])
        gw_hi = sb("gw_hi", [P, 2, E], F32R)
        gw_lo = sb("gw_lo", [P, 2, E], F32R)
        beta_sb = sb("beta_sb", [1, E])
        beta_row = sb("beta_row", [1, G, 2, E])
        S_sb = [sb(f"S_sb{b}", [P, P]) for b in range(B)]
        T1 = [sb(f"T1_{b}", [P, P]) for b in range(B)]
        Gm = [sb(f"Gm{b}", [P, P]) for b in range(B)]
        R_sb = [sb(f"R_sb{b}", [P, P]) for b in range(B)]
        A_sb = [sb(f"A_sb{b}", [P, P]) for b in range(B)]
        xn = [sb(f"xn{u}", [P, G, C]) for u in range(2)]
        st = [sb(f"st{u}", [P, G, 6]) for u in range(2)]
        mv = [sb(f"mv{u}", [P, G, 2]) for u in range(2)]
        vpe = [sb(f"vpe{u}", [P, G]) for u in range(2)]
        rstd = [sb(f"rstd{u}", [P, G]) for u in range(2)]
        nmean = [sb(f"nmean{u}", [P, G]) for u in range(2)]
        shift = [sb(f"shift{u}", [P, G]) for u in range(2)]
        st3 = [sb(f"st3{u}", [P, G, 6]) for u in range(2)]
        mv3 = [sb(f"mv3{u}", [P, G, 2]) for u in range(2)]
        vpe3 = [sb(f"vpe3{u}", [P, G]) for u in range(2)]
        rstd3 = [sb(f"rstd3{u}", [P, G]) for u in range(2)]
        outT = [sb(f"outT{u}", [P, G * P]) for u in range(2)]
        tln = [sb(f"tln{u}", [P, G, C]) for u in range(2)]
        xt = [sb(f"xt{u}", [P, G, C]) for u in range(2)]
        xh = [sb(f"xh{u}", [P, G, P], F32R) for u in range(2)]
        xl = [sb(f"xl{u}", [P, G, P], F32R) for u in range(2)]
        src = [sb(f"src{u}", [P, TOPK, G, ROW]) for u in range(2)]
        slot = [sb(f"slot{u}", [P, G, TOPK], U32) for u in range(2)]
        mx = sb("mx", [P, G, 8])
        ix = sb("ix", [P, G, 8], U32)
        chosen = sb("chosen", [P, G, TOPK, E])
        picked = sb("picked", [P, G, TOPK, E])
        mask = sb("mask", [P, G + 1, E], BF16)
        th = sb("th", [P, G, E])
        weight = sb("weight", [P, G, TOPK])
        place = sb("place", [P, G, E])
        carry = sb("carry", [P, E])
        pad_row = sb("pad_row", [1, E], I32)
        cnt = sb("cnt", [1, E])
        cnti = sb("cnti", [1, E], I32)
        ntiles_i = sb("ntiles_i", [1, E], I32)
        ntiles = sb("ntiles", [1, E])
        ends8 = sb("ends8", [1, E, E])
        ends = sb("ends", [1, E])
        step_of = sb("step_of", [1, E])
        past = sb("past", [1, SLOTS, E])
        past_s = sb("past_s", [1, SLOTS, E])
        exp_f = sb("exp_f", [1, SLOTS])
        exp_i = sb("exp_i", [1, SLOTS], I32)
        row_f = sb("row_f", [1, SLOTS])
        row_g = sb("row_g", [1, SLOTS])
        row_i = sb("row_i", [1, SLOTS], I32)
        rowt = [sb(f"rowt{v}", [P, ROW]) for v in range(UNROLL)]
        rh = [sb(f"rh{v}", [P, P], F32R) for v in range(4)]
        rl = [sb(f"rl{v}", [P, P], F32R) for v in range(4)]
        sgate = [sb(f"sgate{v}", [P, M]) for v in range(2)]
        hid = [sb(f"hid{v}", [P, M]) for v in range(2)]
        hidT = [sb(f"hidT{v}", [P, MC, P]) for v in range(2)]
        eo = [sb(f"eo{v}", [P, C]) for v in range(4)]
        late = gu_f[:].rearrange("p e m -> p (e m)")
        GC = G * C

        def late_view(at, n):
            return late[:, at * GC:(at + n) * GC]

        yin = [late_view(2 * u, 2).rearrange("p (k i c) -> p k i c", k=TOPK, i=G) for u in range(2)]
        z0 = [late_view(4 + u, 1).rearrange("p (i c) -> p i c", i=G) for u in range(2)]
        fo = tln

        bank = [ctx.enter_context(nc.psum_tensor(f"bank{i}", [P, 512], F32)) for i in range(8)]
        xnT_ps = bank[0:2]
        S_ps = bank[2:4]
        prep_ps = bank[4]
        chain_ps = [bank[5 + b][:, 0:P] for b in range(B)]
        LT_ps = bank[7][:, 0:P]
        outT_ps, attn_ps, xtT_ps, small_ps = bank[0], bank[1], bank[2], bank[3]
        lg_ps = small_ps[:, 0:G * 2 * E].rearrange("p (i w e) -> p i w e", i=G, w=2)
        pre_ps = small_ps[:, 128:128 + (G + 1) * E].rearrange("p (i e) -> p i e", i=G + 1)
        rowT_ps = bank[0:2]
        z_ps = bank[0:2]
        gu_ps = bank[4:6]
        hidT_ps = {False: [bank[6][:, 0:M]] * 2, True: [bank[6][:, 0:M], bank[2][:, 0:M]]}
        y_ps = {False: [bank[7][:, 0:C]] * 2, True: [bank[7][:, 0:C], bank[3][:, 0:C]]}

        waits_apart = sem("waits_apart")
        x_in = [sem(f"x_in{q}") for q in range(QS)]
        attn_w_in = sem("attn_w_in")
        metric_in = sem("metric_in")
        router_w_in = sem("router_w_in")
        gu_in = sem("gu_in")
        down_in = sem("down_in")
        zeroed = sem("zeroed")
        consts = sem("consts")
        pool_chain = sem("pool_chain")
        prep_mm = sem("prep_mm")
        prep_sb = sem("prep_sb")
        metric_ready = sem("metric_ready")
        gw_lo_done = sem("gw_lo_done")
        beta_ready = sem("beta_ready")
        gu_hi_done = sem("gu_hi_done")
        gu_lo_done = sem("gu_lo_done")
        st1_w = sem("st1_w")
        mv1_done = sem("mv1_done")
        ln1_c = sem("ln1_c")
        xn_done = sem("xn_done")
        gram_tr = sem("gram_tr")
        xnT_done = sem("xnT_done")
        chain_mm = sem("chain_mm")
        chain_sb = sem("chain_sb")
        gm_done = sem("gm_done")
        outT_mm = sem("outT_mm")
        outT_sb = sem("outT_sb")
        attn_tr = sem("attn_tr")
        st2_w = sem("st2_w")
        mv2_done = sem("mv2_done")
        ln2_c = sem("ln2_c")
        tln_done = sem("tln_done")
        x1_done = sem("x1_done")
        st3_w = sem("st3_w")
        mv3_done = sem("mv3_done")
        ln3_c = sem("ln3_c")
        xt_done = sem("xt_done")
        xtT_tr = sem("xtT_tr")
        xh_done = sem("xh_done")
        xl_done = sem("xl_done")
        logits_mm = sem("logits_mm")
        r1_c = sem("r1_c")
        R1 = 3
        mask_done = sem("mask_done")
        th_done = sem("th_done")
        rb_c = sem("rb_c")
        RB = 2
        prefix_mm = sem("prefix_mm")
        r2_c = sem("r2_c")
        R2 = 3
        src_x_done = sem("src_x_done")
        src_done = sem("src_done")
        rows_out = [sem(f"rows_out{u}") for u in range(2)]
        empty_out = sem("empty_out")
        pads_out = sem("pads_out")
        tab_c = sem("tab_c")
        pad_ready = sem("pad_ready")
        tables = sem("tables")
        gu_mm = sem("gu_mm")
        silu_done = sem("silu_done")
        hid_done = sem("hid_done")
        hidT_tr = sem("hidT_tr")
        hidT_done = sem("hidT_done")
        y_mm = sem("y_mm")
        ysh_done = sem("ysh_done")
        eo_done = sem("eo_done")
        row_in = [sem(f"row_in{v}") for v in range(UNROLL)]
        rowT_tr = sem("rowT_tr")
        rh_done = sem("rh_done")
        rl_done = sem("rl_done")
        res_out = [sem(f"res_out{v}") for v in range(4)]
        y_in = [sem(f"y_in{u}") for u in range(2)]
        z0_done = sem("z0_done")
        z_mm = sem("z_mm")
        st4_w = sem("st4_w")
        mv4_done = sem("mv4_done")
        ln4_c = sem("ln4_c")
        fo_done = sem("fo_done")
        sum_done = sem("sum_done")
        out_sent = [sem(f"out_sent{u}") for u in range(2)]

        block = ctx.enter_context(nc.Block())

        def after(eng, s, value):
            if not isinstance(value, int) or value > 0:
                eng.wait_ge(s, value)

        def wait_apart(eng, s, value):
            eng.wait_ge(s, value)
            if not isinstance(value, int):
                eng.sem_inc(waits_apart, 1)

        def back(q, u, d):
            v = (u - d) % 2
            return q - (d - u + v) // 2, v

        def ahead(q, u):
            return (q, 1) if u == 0 else (q + 1, 0)

        def num(q, u):
            return q * 2 + u

        def exists(q):
            return not isinstance(q, int) or 0 <= q < QS

        def steps(eng, body):
            for u in range(2):
                body(0, u)
            with eng.Fori(1, QS) as q:
                for u in range(2):
                    body(q, u)

        def steps_lagged(eng, body, lag):
            for u in range(2):
                body(0, u)
            with eng.Fori(1, QS - 1) as q:
                for u in range(2):
                    body(q, u)
            for n in range(2 * QS - 2, 2 * QS + lag):
                body(n // 2, n % 2)

        def slots(eng, body, lag):
            for v in range(UNROLL):
                body(v, v)
            with eng.Fori(1, SLOTS // UNROLL - 1) as j:
                for v in range(UNROLL):
                    body(j * UNROLL + v, v)
            for v in range(UNROLL + lag):
                body(SLOTS - UNROLL + v, v % UNROLL)

        def tiles(t, q, u):
            return t[:, u, bass.ds(q * G, G)]

        def bc(ap, axis, shape):
            return ap.unsqueeze(axis).to_broadcast(shape)

        @block.sync
        def _(sp):
            for q in range(QS):
                for u in range(B):
                    sp.dma_start(X[:, u, q * G:(q + 1) * G, :],
                                 x_v[:, u, q * G:(q + 1) * G, :]).then_inc(x_in[q], 16)
            sp.dma_start(gu_f[:, E, 0:M], sg[0]).then_inc(gu_in, 16)
            sp.dma_start(gu_f[:, E, M:2 * M], su[0]).then_inc(gu_in, 16)
            sp.dma_start(gu_f[:, 0:E, 0:M], wg.rearrange("e h m -> h e m")).then_inc(gu_in, 16)
            sp.dma_start(gu_f[:, 0:E, M:2 * M], wu.rearrange("e h m -> h e m")).then_inc(gu_in, 16)
            sp.dma_start(down[:, E, :, :], sd[0].rearrange("(a p) h -> p a h", p=P)).then_inc(down_in, 16)
            for e in range(E):
                sp.dma_start(down[:, e, :, :],
                             wd[e].rearrange("(a p) h -> p a h", p=P)).then_inc(down_in, 16)

            sp.wait_ge(pad_ready, 1)
            for e in range(E):
                row = sp.value_load(pad_row[0:1, e:e + 1], min_val=e * REGION, max_val=e * REGION + T)
                sp.dma_start(rows_d[bass.ds(row, P), :], empty_row[:]).then_inc(pads_out, 16)

            sp.wait_ge(tables, 1)
            for u in range(2):
                sp.wait_ge(rows_out[u], 16 * G * TOPK * QS)
            sp.wait_ge(empty_out, 16)
            sp.wait_ge(pads_out, 16 * E)

            first_row = [sp.alloc_register(f"first_row{v}") for v in range(UNROLL)]

            def load(r, v):
                after(sp, res_out[v % 4], (r - UNROLL + 4) * 4 - (v % 4) * 4)
                row = sp.snap(first_row[v], min_val=0, max_val=EMPTY_REGION)
                sp.dma_start(rowt[v][:, :], rows_d[bass.ds(row, P), :]).then_inc(row_in[v], 16)

            def loads(j):
                sp.reg_load(first_row, row_i[0:1, bass.ds(j * UNROLL, UNROLL)])
                for v in range(UNROLL):
                    load(j * UNROLL + v, v)

            loads(0)
            with sp.Fori(1, SLOTS // UNROLL) as j:
                loads(j)

            for v in range(4):
                sp.wait_ge(res_out[v], 16 * SLOTS // 4)

            def results(q, u):
                after(sp, z0_done, num(q, u) - 1)
                for k in range(TOPK):
                    sp.dma_start(yin[u][:, k],
                                 res_v[:, k, bass.ds(q * G + u * TPB, G), :]).then_inc(y_in[u], 16)

            def output(q, u):
                sp.wait_ge(sum_done, num(q, u) + 1)
                sp.dma_start(tiles(out_v, q, u), fo[u][:]).then_inc(out_sent[u], 16)

            def last(q, u):
                q2, u2 = back(q, u, 2)
                if exists(q):
                    results(q, u)
                if exists(q2):
                    output(q2, u2)

            steps_lagged(sp, last, 2)
            for u in range(2):
                sp.wait_ge(out_sent[u], 16 * QS)

        @block.gpsimd
        def _(gp):
            done = [0]

            def link(ins):
                done[0] += 1
                ins.then_inc(pool_chain, 1)
                gp.wait_ge(pool_chain, done[0])

            nc.gpsimd.memset(ucomp[:], 0.0).then_inc(zeroed, 1)
            nc.gpsimd.memset(mhalf[:], -0.5)
            link(nc.gpsimd.memset(ident[:], 0.0))
            link(nc.gpsimd.affine_select(out=ident[:], in_=ident[:], compare_op=ALU.not_equal, fill=1.0,
                                         base=0, pattern=[[-1, P]], channel_multiplier=1))
            nc.gpsimd.tensor_scalar(centre[:], ident[:], 1.0 / P, None, ALU.subtract)
            nc.gpsimd.memset(ones_row[:], 1.0)
            nc.gpsimd.memset(beta_row[:], 0.0)
            link(nc.gpsimd.memset(headmask[:], 1.0))
            link(nc.gpsimd.affine_select(out=headmask[:], in_=headmask[:], compare_op=ALU.is_ge, fill=0.0,
                                         base=0, pattern=[[-K, H], [0, K]], channel_multiplier=1))
            link(nc.gpsimd.affine_select(out=headmask[:], in_=headmask[:], compare_op=ALU.is_ge, fill=0.0,
                                         base=K - 1, pattern=[[K, H], [0, K]], channel_multiplier=-1))
            nc.gpsimd.memset(ones_b[:], 1.0)
            link(nc.gpsimd.memset(below[:], 1.0))
            link(nc.gpsimd.affine_select(out=below[:], in_=below[:], compare_op=ALU.is_gt, fill=0.0,
                                         base=0, pattern=[[1, P]], channel_multiplier=-1))
            nc.gpsimd.memset(mask[:], 0.0)
            nc.gpsimd.iota(iota8[:], pattern=[[1, E]], base=0, channel_multiplier=0, allow_small_or_imprecise_dtypes=True)
            nc.gpsimd.iota(regbase[:], pattern=[[REGION, E]], base=0, channel_multiplier=0, allow_small_or_imprecise_dtypes=True)
            nc.gpsimd.iota(carry[:], pattern=[[REGION, E]], base=0, channel_multiplier=0, allow_small_or_imprecise_dtypes=True)
            nc.gpsimd.iota(pidx[:], pattern=[[0, 1]], base=0, channel_multiplier=1, allow_small_or_imprecise_dtypes=True)
            nc.gpsimd.iota(iota_t[:], pattern=[[1, SLOTS]], base=0, channel_multiplier=0, allow_small_or_imprecise_dtypes=True)
            nc.gpsimd.iota(ids[:], pattern=[[T, TOPK], [TPB, B], [1, TPB]], base=0,
                           channel_multiplier=TILES)
            for u in range(2):
                nc.gpsimd.memset(src[u][:], 0.0)
            link(nc.gpsimd.memset(upto[:], 1.0))
            link(nc.gpsimd.affine_select(out=upto[:], in_=upto[:], compare_op=ALU.is_ge, fill=0.0,
                                         base=0, pattern=[[1, E], [-1, E]], channel_multiplier=0))
            link(nc.gpsimd.memset(empty_row[:], 0.0))
            link(nc.gpsimd.memset(empty_row[:, P:P + 1].bitcast(I32), NOWHERE))
            nc.gpsimd.dma_start(rows_d[EMPTY_REGION:EMPTY_REGION + P, :], empty_row[:]).then_inc(empty_out, 16)
            gp.engine_nop().then_inc(consts, 1)

            def norm(mv_u, vpe_u, rstd_u, s, base):
                nc.gpsimd.tensor_scalar(vpe_u[:], mv_u[:, :, 1], EPS, None, ALU.add).then_inc(s, 1)
                gp.wait_ge(s, base + 1)
                nc.gpsimd.tensor_tensor(rstd_u[:], vpe_u[:], mhalf[:], ALU.pow).then_inc(s, 1)

            def norm_shift(mv_u, vpe_u, rstd_u, nmean_u, shift_u, s, base):
                nc.gpsimd.tensor_scalar(nmean_u[:], mv_u[:, :, 0], -1.0, None, ALU.mult).then_inc(s, 1)
                norm(mv_u, vpe_u, rstd_u, s, base + 1)
                gp.wait_ge(s, base + 3)
                nc.gpsimd.tensor_tensor(shift_u[:], nmean_u[:], rstd_u[:], ALU.mult).then_inc(s, 1)

            def ln1(q, u):
                after(gp, xn_done, num(q, u) - 1)
                wait_apart(gp, mv1_done, num(q, u) + 1)
                norm_shift(mv[u], vpe[u], rstd[u], nmean[u], shift[u], ln1_c, num(q, u) * 4)

            steps(gp, ln1)

            gp.wait_ge(metric_in, 16 * K)
            nc.gpsimd.tensor_tensor(ubig[:].rearrange("p (h k) -> p h k", h=H),
                                    bc(ucomp[:], 1, [P, H, K]), headmask[:], ALU.mult)
            link(nc.gpsimd.tensor_scalar(iddiag[:], ident[:], dcomp[:], None, ALU.mult))
            nc.gpsimd.tensor_tensor(udiag[:], ubig[:], iddiag[:], ALU.add).then_inc(metric_ready, 1)
            gp.wait_ge(router_w_in, 32)
            nc.gpsimd.tensor_copy(beta_row[:, :, 1, :], bc(beta_sb[:], 1, [1, G, E])).then_inc(beta_ready, 1)

            gp.wait_ge(prep_sb, 2)
            nc.gpsimd.tensor_tensor(gw_lo[:], bc(gwT[:], 1, [P, 2, E]), gw_hi[:].bitcast(F32),
                                    ALU.subtract).then_inc(gw_lo_done, 1)

            def low(n, e):
                gp.wait_ge(gu_hi_done, n + 1)
                nc.gpsimd.tensor_tensor(gu_lo[:, e, :], gu_f[:, e, :], gu_hi[:, e, :].bitcast(F32),
                                        ALU.subtract).then_inc(gu_lo_done, 1)

            low(0, E)

            def scatter(q, u, tiles_of):
                wait_apart(gp, src_x_done, num(q, u) + 1)
                wait_apart(gp, src_done, num(q, u) + 1)
                for i in tiles_of:
                    for k in range(TOPK):
                        nc.gpsimd.indirect_dma_start(
                            rows_d, bass.IndirectOffsetOnAxis(ap=slot[u][:, i, k:k + 1], axis=0),
                            src[u][:, k, i, :], None).then_inc(rows_out[u], 16)

            def attn_step(q, u):
                q2, u2 = back(q, u, 2)
                if exists(q):
                    wait_apart(gp, mv2_done, num(q, u) + 1)
                    norm(mv[u], vpe[u], rstd[u], ln2_c, num(q, u) * 2)
                if exists(q2):
                    scatter(q2, u2, range(0, G // 2))
                if exists(q):
                    wait_apart(gp, mv3_done, num(q, u) + 1)
                    norm(mv3[u], vpe3[u], rstd3[u], ln3_c, num(q, u) * 2)
                if exists(q2):
                    scatter(q2, u2, range(G // 2, G))
                if isinstance(q, int) and q == 0:
                    for e in range(u * E // 2, (u + 1) * E // 2):
                        low(e + 1, e)

            steps_lagged(gp, attn_step, 2)

            def store(r, v):
                wait_apart(gp, eo_done, r + 1)
                nc.gpsimd.indirect_dma_start(
                    res_d, bass.IndirectOffsetOnAxis(ap=rowt[v][:, P:P + 1].bitcast(U32), axis=0),
                    eo[v % 4][:], None, bounds_check=TOPK * T - 1, oob_is_err=False
                ).then_inc(res_out[v % 4], 16)

            slots(gp, store, 0)

            def last(q, u):
                after(gp, fo_done, num(q, u) - 1)
                wait_apart(gp, mv4_done, num(q, u) + 1)
                norm_shift(mv[u], vpe[u], rstd[u], nmean[u], shift[u], ln4_c, num(q, u) * 4)

            steps(gp, last)

        def silu(act, g, v):
            act.wait_ge(gu_mm, g + 1)
            after(act, hid_done, g - 1)
            nc.scalar.activation(sgate[v][:], gu_ps[v][:, 0:M], ACT.Silu).then_inc(silu_done, 1)

        def hidT_copy(act, g, v, own=False):
            if isinstance(g, int) and g < 0:
                return
            act.wait_ge(hidT_tr, g + 1)
            after(act, y_mm, g - 1)
            nc.scalar.activation(hidT[v][:].rearrange("p a t -> p (a t)"), hidT_ps[own][v],
                                 ACT.Copy).then_inc(hidT_done, 1)

        @block.scalar
        def _(act):
            act.dma_start(Wc[:], proj[0].rearrange("n c k -> c n k")).then_inc(attn_w_in, 16)
            act.dma_start(mix[:], mixer_w).then_inc(attn_w_in, 16)
            act.dma_start(mixb[:], mixer_b.rearrange("(c a) -> c a", a=1), allow_slow_non_contiguous=True).then_inc(attn_w_in, 16)
            act.dma_start(gw[:], gate_w).then_inc(router_w_in, 16)
            act.dma_start(beta_sb[:], beta.rearrange("(a e) -> a e", a=1)).then_inc(router_w_in, 16)
            act.wait_ge(zeroed, 1)
            act.dma_start(dcomp[:], diag.rearrange("h (k a) -> (h k) a", a=1), allow_slow_non_contiguous=True).then_inc(metric_in, 16)
            off = 0
            for k in range(K - 1):
                act.dma_start(ucomp[k:P:K, k + 1:K], halves[:, off:off + K - 1 - k],
                              allow_slow_non_contiguous=True).then_inc(metric_in, 16)
                off += K - 1 - k

            def first(q, u):
                act.wait_ge(ln1_c, num(q, u) * 4 + 4)
                after(act, gram_tr, num(q, u) - 1)
                for i in range(G):
                    last = nc.scalar.activation(xn[u][:, i, :], X[:, u, bass.ds(q * G + i, 1), :].rearrange("p a c -> p (a c)"),
                                                ACT.Identity, bias=shift[u][:, i:i + 1], scale=rstd[u][:, i:i + 1])
                last.then_inc(xn_done, 1)

            steps(act, first)

            act.wait_ge(prep_mm, 1)
            nc.scalar.activation(WT[:], prep_ps[:, 0:128], ACT.Copy)
            nc.scalar.activation(mixT[:], prep_ps[:, 128:256], ACT.Copy)
            nc.scalar.activation(mixb_c[:], prep_ps[:, 256 + E:257 + E], ACT.Copy)
            nc.scalar.activation(gwT[:], prep_ps[:, 256:256 + E], ACT.Copy).then_inc(prep_sb, 1)
            act.wait_ge(prep_sb, 1)
            nc.scalar.activation(gw_hi[:], bc(gwT[:], 1, [P, 2, E]), ACT.Copy).then_inc(prep_sb, 1)

            act.wait_ge(gram_tr, STEPS)
            for b in range(B):
                nc.scalar.activation(S_sb[b][:], S_ps[b][:, 0:P], ACT.Copy).then_inc(chain_sb, 1)
            act.wait_ge(prep_mm, 2)
            nc.scalar.activation(LT[:], LT_ps, ACT.Copy).then_inc(prep_sb, 1)
            for n, dst in ((0, T1), (2, R_sb), (3, A_sb)):
                for b in range(B):
                    act.wait_ge(chain_mm, n * B + b + 1)
                    nc.scalar.activation(dst[b][:], chain_ps[b], ACT.Copy).then_inc(chain_sb, 1)

            def high(e):
                nc.scalar.activation(gu_hi[:, e, :], gu_f[:, e, :], ACT.Copy).then_inc(gu_hi_done, 1)

            act.wait_ge(gu_in, 64)
            high(E)

            def unit(q, u, i):
                g = num(q, u) * G + i
                silu(act, g, i % 2)
                hidT_copy(act, g - 1, (i - 1) % 2)
                ysh_copy(q, u, i - 2)

            def ysh_copy(q, u, i):
                if i < 0:
                    q, u = back(q, u, 1)
                    i += G
                    if not exists(q):
                        return
                g = num(q, u) * G + i
                act.wait_ge(y_mm, g + 1)
                nc.scalar.activation(ysh[:, u, bass.ds(q * G + i, 1), :].rearrange("p a c -> p (a c)"),
                                     y_ps[False][i % 2], ACT.Copy).then_inc(ysh_done, 1)

            def attention_T(q, u):
                s = num(q, u)
                act.wait_ge(outT_mm, s + 1)
                after(act, attn_tr, s - 1)
                nc.scalar.activation(outT[u][:], outT_ps[:, :], ACT.Identity, bias=mixb_c[:]).then_inc(outT_sb, 1)

            def attn_step(q, u):
                q1, u1 = back(q, u, 1)
                q2, u2 = back(q, u, 2)
                qa, ua = ahead(q, u)
                if exists(q2):
                    unit(q2, u2, 2)
                if exists(q1):
                    s = num(q1, u1)
                    act.wait_ge(xtT_tr, s + 1)
                    after(act, gu_mm, (s - 1) * G)
                    nc.scalar.activation(xh[u1][:].rearrange("p i t -> p (i t)"), xtT_ps[:, :],
                                         ACT.Copy).then_inc(xh_done, 1)
                if exists(q2):
                    unit(q2, u2, 3)
                if exists(q):
                    s = num(q, u)
                    act.wait_ge(ln2_c, s * 2 + 2)
                    after(act, x1_done, s - 1)
                    for i in range(G):
                        last = nc.scalar.activation(tln[u][:, i, :], attn_ps[:, i * P:(i + 1) * P], ACT.Copy,
                                                    scale=rstd[u][:, i:i + 1])
                    last.then_inc(tln_done, 1)
                if exists(q1):
                    s = num(q1, u1)
                    act.wait_ge(logits_mm, s + 1)
                    after(act, rb_c, s * RB)
                    nc.scalar.activation(th[:], lg_ps[:, :, 0, :], ACT.Tanh, scale=0.5).then_inc(th_done, 1)
                if exists(qa):
                    attention_T(qa, ua)
                if exists(q1):
                    unit(q1, u1, 0)
                    after(act, rows_out[u1], q1 * 16 * G * TOPK)
                    for k in range(TOPK):
                        last = nc.scalar.activation(src[u1][:, k, :, 0:P], xt[u1][:], ACT.Copy)
                    last.then_inc(src_x_done, 1)
                    unit(q1, u1, 1)
                if isinstance(q, int) and q == 0:
                    for e in range(u * E // 2, (u + 1) * E // 2):
                        high(e)

            attention_T(0, 0)
            steps_lagged(act, attn_step, 2)
            hidT_copy(act, TILES - 1, 1)
            ysh_copy(QS - 1, 1, 2)
            ysh_copy(QS - 1, 1, 3)

            def row_high(r, v):
                act.wait_ge(rowT_tr, r + 1)
                after(act, gu_mm, r - 4 + TILES + 1 if not isinstance(r, int) or r >= 4 else 0)
                nc.scalar.activation(rh[v % 4][:], rowT_ps[v % 2][:, 0:P], ACT.Copy).then_inc(rh_done, 1)

            def routed(r, v):
                if not isinstance(r, int) or r < SLOTS:
                    silu(act, r + TILES, v % 2)
                if not isinstance(r, int) or r + 2 < SLOTS:
                    row_high(r + 2, (v + 2) % UNROLL)
                if not isinstance(r, int) or 1 <= r <= SLOTS:
                    hidT_copy(act, r - 1 + TILES, (v - 1) % 2, True)

            row_high(0, 0)
            row_high(1, 1)
            slots(act, routed, 1)

            def last_step(q, u):
                s = num(q, u)
                act.wait_ge(ln4_c, s * 4 + 4)
                after(act, out_sent[u], q * 16)
                for i in range(G):
                    last = nc.scalar.activation(fo[u][:, i, :], z_ps[u][:, i * P:(i + 1) * P], ACT.Identity,
                                                bias=shift[u][:, i:i + 1], scale=rstd[u][:, i:i + 1])
                last.then_inc(fo_done, 1)

            steps(act, last_step)

        @block.vector
        def _(dve):
            dve.wait_ge(consts, 1)

            def stats(src_of, st_u, mv_u, st_sem, mv_sem, s):
                for i in range(G):
                    last = nc.vector.bn_stats(st_u[:, i, :], src_of(i))
                last.then_inc(st_sem, 1)
                wait_apart(dve, st_sem, s + 1)
                for i in range(G):
                    last = nc.vector.bn_aggr(mv_u[:, i, :], st_u[:, i, :])
                last.then_inc(mv_sem, 1)

            def xnT_copy(q, u):
                s = num(q, u)
                dve.wait_ge(gram_tr, s + 1)
                nc.vector.tensor_copy(xnT[:, u, bass.ds(q * G * P, G * P)], xnT_ps[u][:, :]).then_inc(xnT_done, 1)

            def make_metric():
                dve.wait_ge(metric_ready, 1)
                dve.wait_ge(prep_sb, 1)
                nc.vector.tensor_tensor(metric[:], prep_ps[:, 384:512], udiag[:], ALU.add).then_inc(metric_ready, 1)

            for q in range(QS):
                dve.wait_ge(x_in[q], 32)
                for u in range(2):
                    s = num(q, u)
                    after(dve, ln1_c, (s - 1) * 4)
                    stats(lambda i: X[:, u, q * G + i, :], st[u], mv[u], st1_w, mv1_done, s)
                if q >= 1:
                    for u in range(2):
                        xnT_copy(q - 1, u)
            for u in range(2):
                xnT_copy(QS - 1, u)
            make_metric()
            for b in range(B):
                dve.wait_ge(chain_mm, B + b + 1)
                nc.vector.tensor_tensor(Gm[b][:], chain_ps[b], headmask[:].rearrange("p h k -> p (h k)"), ALU.mult).then_inc(gm_done, 1)

            def hidden(g, v):
                dve.wait_ge(silu_done, g + 1)
                after(dve, hidT_tr, g - 1)
                nc.vector.tensor_tensor(hid[v][:], sgate[v][:], gu_ps[v][:, M:2 * M], ALU.mult).then_inc(hid_done, 1)

            def normalise(q, u):
                s = num(q, u)
                dve.wait_ge(ln3_c, s * 2 + 2)
                after(dve, src_x_done, s - 1)
                for i in range(G):
                    last = nc.vector.tensor_scalar(xt[u][:, i, :], x1[:, u, bass.ds(q * G + i, 1), :].rearrange("p a c -> p (a c)"),
                                                   mv3[u][:, i, 0:1], rstd3[u][:, i:i + 1], ALU.subtract, ALU.mult)
                last.then_inc(xt_done, 1)

            def low_part(q, u):
                dve.wait_ge(xh_done, num(q, u) + 1)
                nc.vector.tensor_tensor(xl[u][:].rearrange("p i t -> p (i t)"), xtT_ps[:, :],
                                        xh[u][:].rearrange("p i t -> p (i t)").bitcast(F32),
                                        ALU.subtract).then_inc(xl_done, 1)

            def choose(q, u):
                s = num(q, u)
                n = [0]

                def link(ins):
                    n[0] += 1
                    ins.then_inc(r1_c, 1)
                    wait_apart(dve, r1_c, s * R1 + n[0])

                wait_apart(dve, th_done, s + 1)
                for i in range(G):
                    last = nc.vector.max(mx[:, i, :], lg_ps[:, i, 1, :])
                link(last)
                for i in range(G):
                    last = nc.vector.max_index(ix[:, i, :], mx[:, i, :], lg_ps[:, i, 1, :])
                link(last)
                link(nc.vector.tensor_tensor(chosen[:], iota8[:].unsqueeze(1).unsqueeze(1).to_broadcast([P, G, TOPK, E]),
                                             bc(ix[:, :, 0:TOPK], 3, [P, G, TOPK, E]), ALU.is_equal))
                assert n[0] == R1
                after(dve, prefix_mm, s)
                nc.vector.tensor_tensor(mask[:, 0:G, :], chosen[:, :, 0, :], chosen[:, :, 1, :],
                                        ALU.add).then_inc(mask_done, 1)

            def probabilities(q, u):
                s = num(q, u)
                nc.vector.tensor_tensor(picked[:], chosen[:], bc(th[:], 2, [P, G, TOPK, E]),
                                        ALU.mult).then_inc(rb_c, 1)
                dve.wait_ge(rb_c, s * RB + 1)
                nc.vector.tensor_reduce(weight[:], picked[:], axis=AX.X, op=ALU.add).then_inc(rb_c, 1)

            def places(q, u):
                s = num(q, u)
                dve.wait_ge(prefix_mm, s + 1)
                nc.vector.tensor_tensor(place[:], pre_ps[:, 0:G, :], bc(carry[:], 1, [P, G, E]),
                                        ALU.add).then_inc(r2_c, 1)
                dve.wait_ge(rb_c, s * RB + RB)
                after(dve, rows_out[u], q * 16 * G * TOPK)
                nc.vector.tensor_scalar(src[u][:, :, :, P + 1:P + 2].rearrange("p k i a -> p k (i a)"),
                                        weight[:].rearrange("p i k -> p k i"), 0.5, 0.5, ALU.mult, ALU.add)
                dve.wait_ge(r2_c, s * R2 + 1)
                nc.vector.tensor_tensor(picked[:], chosen[:], bc(place[:], 2, [P, G, TOPK, E]),
                                        ALU.mult).then_inc(r2_c, 1)
                nc.vector.tensor_copy(src[u][:, :, :, P:P + 1].rearrange("p k i a -> p k (i a)").bitcast(I32),
                                      ids[:, :, u, bass.ds(q * G, G)])
                dve.wait_ge(r2_c, s * R2 + 2)
                nc.vector.tensor_tensor(carry[:], carry[:], pre_ps[:, G, :], ALU.add).then_inc(r2_c, 1)
                with nc.allow_low_precision(reason="whole numbers below 2 ** 24"):
                    nc.vector.tensor_reduce(slot[u][:], picked[:], axis=AX.X, op=ALU.add).then_inc(src_done, 1)
                dve.wait_ge(r2_c, s * R2 + R2)

            def attn_step(q, u):
                q1, u1 = back(q, u, 1)
                q2, u2 = back(q, u, 2)
                if exists(q):
                    s = num(q, u)
                    dve.wait_ge(attn_tr, s + 1)
                    after(dve, ln2_c, (s - 1) * 2)
                    stats(lambda i: attn_ps[:, i * P:(i + 1) * P], st[u], mv[u], st2_w, mv2_done, s)
                if exists(q2):
                    hidden(num(q2, u2) * G + 2, 0)
                if exists(q1):
                    normalise(q1, u1)
                if exists(q2):
                    hidden(num(q2, u2) * G + 3, 1)
                if exists(q1):
                    low_part(q1, u1)
                if exists(q):
                    dve.wait_ge(tln_done, s + 1)
                    nc.vector.tensor_tensor(tiles(x1, q, u), tln[u][:], tiles(X, q, u), ALU.add).then_inc(x1_done, 1)
                    wait_apart(dve, x1_done, s + 1)
                    stats(lambda i: x1[:, u, bass.ds(q * G + i, 1), :].rearrange("p a c -> p (a c)"),
                          st3[u], mv3[u], st3_w, mv3_done, s)
                if exists(q1):
                    choose(q1, u1)
                    hidden(num(q1, u1) * G, 0)
                    probabilities(q1, u1)
                    hidden(num(q1, u1) * G + 1, 1)
                    places(q1, u1)

            steps_lagged(dve, attn_step, 2)

            n = [0]

            def link(ins):
                n[0] += 1
                ins.then_inc(tab_c, 1)
                dve.wait_ge(tab_c, n[0])

            nc.vector.tensor_copy(pad_row[:], carry[0:1, :]).then_inc(pad_ready, 1)
            link(nc.vector.tensor_tensor(cnt[:], carry[0:1, :], regbase[0:1, :], ALU.subtract))
            link(nc.vector.tensor_scalar(cnti[:], cnt[:], float(P - 1), None, ALU.add))
            link(nc.vector.tensor_scalar(ntiles_i[:], cnti[:], 7, None, ALU.logical_shift_right))
            link(nc.vector.tensor_copy(ntiles[:], ntiles_i[:]))
            nc.vector.tensor_scalar(step_of[:], ntiles[:], float(-P), float(REGION), ALU.mult, ALU.add)
            link(nc.vector.tensor_tensor(ends8[:], upto[:], bc(ntiles[:], 1, [1, E, E]), ALU.mult))
            link(nc.vector.tensor_reduce(ends[:], ends8[:], axis=AX.X, op=ALU.add))
            link(nc.vector.tensor_tensor(past[:], bc(iota_t[:], 2, [1, SLOTS, E]), bc(ends[:], 1, [1, SLOTS, E]),
                                         ALU.is_ge))
            nc.vector.tensor_tensor(past_s[:], past[:], bc(step_of[:], 1, [1, SLOTS, E]), ALU.mult)
            link(nc.vector.tensor_reduce(exp_f[:], past[:], axis=AX.X, op=ALU.add))
            nc.vector.tensor_scalar(exp_i[:], exp_f[:], float(E - 1), None, ALU.min)
            link(nc.vector.tensor_reduce(row_f[:], past_s[:], axis=AX.X, op=ALU.add))
            link(nc.vector.scalar_tensor_tensor(out=row_g[:], in0=iota_t[:], scalar=float(P), in1=row_f[:],
                                                op0=ALU.mult, op1=ALU.add))
            nc.vector.tensor_scalar(row_i[:], row_g[:], float(EMPTY_REGION), None, ALU.min).then_inc(tables, 1)

            def row_low(r, v):
                dve.wait_ge(rh_done, r + 1)
                nc.vector.tensor_tensor(rl[v % 4][:], rowT_ps[v % 2][:, 0:P], rh[v % 4][:].bitcast(F32),
                                        ALU.subtract).then_inc(rl_done, 1)

            def routed(r, v):
                if not isinstance(r, int) or r < SLOTS:
                    hidden(r + TILES, v % 2)
                if not isinstance(r, int) or r + 2 < SLOTS:
                    row_low(r + 2, (v + 2) % UNROLL)
                if not isinstance(r, int) or r >= 2:
                    w = (v - 2) % UNROLL
                    dve.wait_ge(y_mm, r - 2 + TILES + 1)
                    after(dve, res_out[w % 4], (r - 2 - w % 4) * 4)
                    nc.vector.tensor_scalar(eo[w % 4][:], y_ps[True][w % 2], rowt[w][:, P + 1:P + 2], None,
                                            ALU.mult).then_inc(eo_done, 1)

            row_low(0, 0)
            row_low(1, 1)
            slots(dve, routed, 2)

            def last_step(q, u):
                q1, u1 = back(q, u, 1)
                q2, u2 = back(q, u, 2)
                if exists(q):
                    dve.wait_ge(y_in[u], q * 32 + 32)
                    after(dve, z_mm, num(q, u) - 1)
                    nc.vector.tensor_tensor(z0[u][:], yin[u][:, 0], yin[u][:, 1], ALU.add).then_inc(z0_done, 1)
                if exists(q1):
                    s = num(q1, u1)
                    wait_apart(dve, z_mm, s + 1)
                    after(dve, ln4_c, (s - 1) * 4)
                    stats(lambda i: z_ps[u1][:, i * P:(i + 1) * P], st[u1], mv[u1], st4_w, mv4_done, s)
                if exists(q2):
                    dve.wait_ge(fo_done, num(q2, u2) + 1)
                    nc.vector.tensor_tensor(fo[u2][:], fo[u2][:], tiles(x1, q2, u2), ALU.add).then_inc(sum_done, 1)

            steps_lagged(dve, last_step, 2)

        @block.tensor
        def _(pe):
            mm = nc.tensor.matmul
            pe.wait_ge(consts, 1)
            def first(q, u):
                s = num(q, u)
                pe.wait_ge(xn_done, s + 1)
                after(pe, xnT_done, s - 1)
                for i in range(G):
                    mm(S_ps[u][:, 0:P], xn[u][:, i, :], xn[u][:, i, :], start=isinstance(q, int) and i == 0,
                       stop=i == G - 1, skip_group_check=True)
                for i in range(G):
                    last = nc.tensor.transpose(xnT_ps[u][:, i * P:(i + 1) * P], xn[u][:, i, :], ident[:])
                last.then_inc(gram_tr, 1)

            steps(pe, first)

            Wf = Wc[:].rearrange("p h k -> p (h k)")
            pe.wait_ge(attn_w_in, 48)
            pe.wait_ge(router_w_in, 32)
            pe.wait_ge(metric_ready, 1)
            nc.tensor.transpose(prep_ps[:, 0:128], Wf, ident[:])
            mm(prep_ps[:, 128:256], mix[:], centre[:], start=True, stop=True)
            nc.tensor.transpose(prep_ps[:, 256:256 + E], gw[:], ident[0:E, 0:E])
            mm(prep_ps[:, 256 + E:257 + E], centre[:], mixb[:], start=True, stop=True)
            nc.tensor.transpose(prep_ps[:, 384:512], ubig[:], ident[:]).then_inc(prep_mm, 1)

            pe.wait_ge(metric_ready, 2)
            pe.wait_ge(prep_sb, 1)
            mm(LT_ps, metric[:], WT[:], start=True, stop=True).then_inc(prep_mm, 1)
            pe.wait_ge(prep_sb, 3)

            for lhs, rhs, ready, at in ((S_sb, None, chain_sb, 0), (None, T1, chain_sb, B),
                                        (Gm, mixT, gm_done, 0), (LT, R_sb, chain_sb, 2 * B)):
                for b in range(B):
                    pe.wait_ge(ready, at + b + 1)
                    left = Wf if lhs is None else lhs[:] if lhs is LT else lhs[b][:]
                    right = Wf if rhs is None else rhs[:] if rhs is mixT else rhs[b][:]
                    mm(chain_ps[b], left, right, start=True, stop=True).then_inc(chain_mm, 1)
            pe.wait_ge(chain_sb, 4 * B)
            pe.wait_ge(xnT_done, STEPS)

            def gate_up(g, v, hi, lo, e):
                after(pe, hid_done, g - 1)
                mm(gu_ps[v][:, :], hi, gu_hi[:, e, :], start=True, stop=False)
                mm(gu_ps[v][:, :], hi, gu_lo[:, e, :], start=False, stop=False)
                mm(gu_ps[v][:, :], lo, gu_hi[:, e, :], start=False, stop=True).then_inc(gu_mm, 1)

            def hidden_T(g, v, own=False):
                if isinstance(g, int) and g < 0:
                    return
                pe.wait_ge(hid_done, g + 1)
                after(pe, hidT_done, g - 1 if own else g)
                for a in range(MC):
                    last = nc.tensor.transpose(hidT_ps[own][v][:, a * P:(a + 1) * P], hid[v][:, a * P:(a + 1) * P], ident[:])
                last.then_inc(hidT_tr, 1)

            def result(g, v, e, own=False):
                pe.wait_ge(hidT_done, g + 1)
                for a in range(MC):
                    last = mm(y_ps[own][v], hidT[v][:, a, :], down[:, e, a, :], start=a == 0, stop=a == MC - 1)
                last.then_inc(y_mm, 1)

            def shared(q, u, i):
                g = num(q, u) * G + i
                gate_up(g, i % 2, xh[u][:, i, :], xl[u][:, i, :], E)
                hidden_T(g - 1, (i - 1) % 2)
                if not isinstance(g, int) or g >= 2:
                    after(pe, ysh_done, g - 2)
                    result(g - 2, i % 2, E)

            def attention_T(q, u):
                s = num(q, u)
                after(pe, outT_sb, s)
                mm(outT_ps[:, :], A_sb[u][:], xnT[:, u, bass.ds(q * G * P, G * P)], start=True,
                   stop=True).then_inc(outT_mm, 1)

            def attention(q, u):
                s = num(q, u)
                pe.wait_ge(outT_sb, s + 1)
                after(pe, tln_done, s)
                for i in range(G):
                    last = nc.tensor.transpose(attn_ps[:, i * P:(i + 1) * P], outT[u][:, i * P:(i + 1) * P], ident[:])
                last.then_inc(attn_tr, 1)

            def attn_step(q, u):
                q1, u1 = back(q, u, 1)
                q2, u2 = back(q, u, 2)
                qa, ua = ahead(q, u)
                s1 = num(q1, u1)
                if exists(q2):
                    shared(q2, u2, 2)
                if exists(q1):
                    pe.wait_ge(xt_done, s1 + 1)
                    after(pe, xl_done, s1)
                    for i in range(G):
                        last = nc.tensor.transpose(xtT_ps[:, i * P:(i + 1) * P], xt[u1][:, i, :], ident[:])
                    last.then_inc(xtT_tr, 1)
                if exists(q2):
                    shared(q2, u2, 3)
                if exists(q1):
                    if isinstance(s1, int) and s1 == 0:
                        pe.wait_ge(gw_lo_done, 1)
                        pe.wait_ge(beta_ready, 1)
                        pe.wait_ge(gu_lo_done, 1)
                        pe.wait_ge(down_in, 16 * (E + 1))
                    after(pe, r2_c, s1 * R2)
                    mm(small_ps[:, 0:G * 2 * E], ones_row[:], beta_row[:].rearrange("a i w e -> a (i w e)"),
                       start=True, stop=False, skip_group_check=True)
                    pe.wait_ge(xl_done, s1 + 1)
                    for i in range(G):
                        for x_part, w_part in ((xh, gw_hi), (xh, gw_lo), (xl, gw_hi), (xl, gw_lo)):
                            last = mm(lg_ps[:, i].rearrange("p w e -> p (w e)"), x_part[u1][:, i, :],
                                      w_part[:].rearrange("p w e -> p (w e)"), start=False,
                                      stop=w_part is gw_lo and x_part is xl, skip_group_check=True)
                    last.then_inc(logits_mm, 1)
                if exists(qa):
                    attention_T(qa, ua)
                if exists(q1):
                    shared(q1, u1, 0)
                if exists(qa):
                    attention(qa, ua)
                if exists(q1):
                    shared(q1, u1, 1)
                    pe.wait_ge(mask_done, s1 + 1)
                    mm(pre_ps, below[:], mask[:], start=True, stop=False)
                    for i in range(G):
                        last = mm(pre_ps[:, i + 1:G + 1, :], ones_b[:], bc(mask[:, i, :], 1, [P, G - i, E]),
                                  start=False, stop=i == G - 1)
                    last.then_inc(prefix_mm, 1)

            attention_T(0, 0)
            attention(0, 0)
            steps_lagged(pe, attn_step, 2)
            hidden_T(TILES - 1, 1)
            pe.wait_ge(ysh_done, TILES - 2)
            result(TILES - 2, 0, E)
            pe.wait_ge(ysh_done, TILES - 1)
            result(TILES - 1, 1, E)
            pe.wait_ge(ysh_done, TILES)

            pe.wait_ge(tables, 1)
            pe.wait_ge(gu_lo_done, E + 1)

            def row_T(r, v):
                pe.wait_ge(row_in[v], (r - v) * 2 + 16)
                after(pe, rl_done, r - 1)
                nc.tensor.transpose(rowT_ps[v % 2][:, 0:P], rowt[v][:, 0:P], ident[:]).then_inc(rowT_tr, 1)

            own = [pe.alloc_register(f"expert{k}") for k in range(UNROLL + 2)]
            coming = [pe.alloc_register(f"next_expert{k}") for k in range(UNROLL)]

            def expert(v):
                return bass.ds(pe.snap(own[v + 2], min_val=0, max_val=E - 1), 1)

            def block_turns(j):
                for k in range(2):
                    pe.reg_mov(own[k], own[UNROLL + k])
                for k in range(UNROLL):
                    pe.reg_mov(own[k + 2], coming[k])

            def routed(r, v):
                if not isinstance(r, int) or r < SLOTS:
                    e = expert(v)
                    pe.wait_ge(rl_done, r + 1)
                    gate_up(r + TILES, v % 2, rh[v % 4][:], rl[v % 4][:], e)
                if not isinstance(r, int) or r + 2 < SLOTS:
                    row_T(r + 2, (v + 2) % UNROLL)
                if v == 4 and (not isinstance(r, int) or r + UNROLL < SLOTS):
                    pe.reg_load(coming, exp_i[0:1, bass.ds(r + (UNROLL - 4), UNROLL)])
                if not isinstance(r, int) or 1 <= r <= SLOTS:
                    hidden_T(r - 1 + TILES, (v - 1) % 2, True)
                if not isinstance(r, int) or r >= 2:
                    e = expert(v - 2)
                    after(pe, eo_done, r - 3)
                    result(r - 2 + TILES, v % 2, e, True)

            def block_of(j, n):
                block_turns(j)
                for v in range(n):
                    routed(j * UNROLL + v, v)

            row_T(0, 0)
            row_T(1, 1)
            for k in range(2):
                pe.reg_mov(own[UNROLL + k], 0)
            pe.reg_load(coming, exp_i[0:1, 0:UNROLL])
            block_of(0, UNROLL)
            with pe.Fori(1, SLOTS // UNROLL - 1) as j:
                block_of(j, UNROLL)
            block_of(SLOTS // UNROLL - 1, UNROLL)
            routed(SLOTS, UNROLL)
            routed(SLOTS + 1, UNROLL + 1)

            def last_step(q, u):
                s = num(q, u)
                pe.wait_ge(z0_done, s + 1)
                after(pe, fo_done, s - 1)
                mm(z_ps[u][:, :], ident[:], z0[u].rearrange("p i c -> p (i c)"), start=True, stop=False)
                mm(z_ps[u][:, :], ident[:], tiles(ysh, q, u).rearrange("p i c -> p (i c)"), start=False,
                   stop=True).then_inc(z_mm, 1)

            steps(pe, last_step)


_INS = ["L0_attn_in_sequence_bwc", "L0_attn_projection_1nck", "L0_attn_halves", "L0_attn_diagonals_nk",
        "L0_attn_mixer_w", "L0_attn_mixer_b", "L0_ffn_gate_w", "L0_ffn_beta", "L0_ffn_gate_proj_w",
        "L0_ffn_up_proj_w", "L0_ffn_down_proj_w", "L0_ffn_shared_gate_w", "L0_ffn_shared_up_w",
        "L0_ffn_shared_down_w"]


def kernel(**inputs):
    import numpy as np
    import concourse.bacc as bacc
    from concourse.bass_utils import run_bass_kernel_spmd

    nc = bacc.Bacc("TRN2", target_bir_lowering=False, num_devices=1)
    arrays, args = {}, []
    for name in _INS:
        a = np.ascontiguousarray(inputs[name])
        arrays[f"in_{name}"] = a
        args.append(nc.dram_tensor(f"in_{name}", a.shape, mybir.dt.from_np(a.dtype), kind="ExternalInput").ap())
    shape = inputs[_INS[0]].shape
    args.append(nc.dram_tensor("out_0", shape, F32, kind="ExternalOutput").ap())
    build_sandwich(nc, *args)
    r = run_bass_kernel_spmd(nc, [arrays], core_ids=[0])
    return r.results[0]["out_0"]
```

```python
from contextlib import ExitStack

import concourse.bass as bass
from concourse import mybir

F32 = mybir.dt.float32
F32R = mybir.dt.float32r
BF16 = mybir.dt.bfloat16
I32 = mybir.dt.int32
U32 = mybir.dt.uint32
ALU = mybir.AluOpType
ACT = mybir.ActivationFunctionType
AX = mybir.AxisListType

P = 128
G = 4
EPS = 1e-5
TOPK = 2


def build_sandwich(nc, x, proj, halves, diag, mixer_w, mixer_b, gate_w, beta,
                   wg, wu, wd, sg, su, sd, out):
    B, W, C = x.shape
    H, K = diag.shape
    E, _, M = wg.shape
    MC = M // P
    TPB = W // P
    TILES = B * TPB
    QS = TPB // G
    STEPS = B * QS
    T = B * W
    assert C == P and H * K == P and B == 2 and TOPK * M == 4 * P

    REGION = T + P
    ROW = P + 4
    EMPTY_REGION = E * REGION
    RING = 4
    UNROLL = 12
    SLOTS = -(-((TOPK * T + E * (P - 1)) // P) // UNROLL) * UNROLL
    NOWHERE = TOPK * T

    x_v = x.rearrange("b (p j) c -> p b j c", p=P)
    out_v = out.rearrange("b (p j) c -> p b j c", p=P)

    with ExitStack() as ctx:
        def sb(name, shape, dt=F32):
            return ctx.enter_context(nc.sbuf_tensor(name, shape, dt))

        def sem(name):
            return ctx.enter_context(nc.semaphore(name))

        rows_d = nc.dram_tensor("expert_rows", [EMPTY_REGION + P, ROW], F32).ap()
        res_d = nc.dram_tensor("expert_results", [TOPK * T, C], F32).ap()
        res_v = res_d.rearrange("(k p t) c -> p k t c", k=TOPK, p=P)

        X = sb("X", [P, B, TPB, C])
        xnT = sb("xnT", [P, B, TPB * P])
        x1 = sb("x1", [P, B, TPB, C])
        ysh = sb("ysh", [P, B, TPB, C])
        ids = sb("ids", [P, TOPK, B, TPB], I32)
        gu_f = sb("gu_f", [P, E + 1, 2 * M])
        gu_hi = sb("gu_hi", [P, E + 1, 2 * M], F32R)
        gu_lo = sb("gu_lo", [P, E + 1, 2 * M], F32R)
        down = sb("down", [P, E + 1, MC, C])
        down_mean = sb("down_mean", [P, E + 1, MC])
        ident = sb("ident", [P, P])
        headmask = sb("headmask", [P, H, K])
        below = sb("below", [P, P], BF16)
        ones_b = sb("ones_b", [P, P], BF16)
        iota8 = sb("iota8", [P, E])
        centre = sb("centre", [P, P])
        ones_row = sb("ones_row", [1, P])
        iota_t = sb("iota_t", [1, SLOTS])
        upto = sb("upto", [1, E, E])
        regbase = sb("regbase", [P, E])
        mhalf = sb("mhalf", [P, G])
        table_in = sb("table_in", [P, G])
        empty_row = sb("empty_row", [P, ROW])
        Wc = sb("Wc", [P, H, K])
        WT = sb("WT", [P, P])
        mix = sb("mix", [P, C])
        mixT = sb("mixT", [P, C])
        mixb = sb("mixb", [P, 1])
        mixb_c = sb("mixb_c", [P, 1])
        ucomp = sb("ucomp", [P, K])
        dcomp = sb("dcomp", [P, 1])
        ubig = sb("ubig", [P, P])
        udiag = sb("udiag", [P, P])
        iddiag = sb("iddiag", [P, P])
        metric = sb("metric", [P, P])
        LT = sb("LT", [P, P])
        gw = sb("gw", [E, C])
        gwT = sb("gwT", [P, E])
        gw_hi = sb("gw_hi", [P, 2, E], F32R)
        gw_lo = sb("gw_lo", [P, 2, E], F32R)
        beta_sb = sb("beta_sb", [1, E])
        beta_row = sb("beta_row", [1, G, 2, E])
        S_sb = [sb(f"S_sb{b}", [P, P]) for b in range(B)]
        T1 = [sb(f"T1_{b}", [P, P]) for b in range(B)]
        Gm = [sb(f"Gm{b}", [P, P]) for b in range(B)]
        R_sb = [sb(f"R_sb{b}", [P, P]) for b in range(B)]
        A_sb = [sb(f"A_sb{b}", [P, P]) for b in range(B)]
        st = [sb(f"st{u}", [P, G, 6]) for u in range(RING)]
        mv = [sb(f"mv{u}", [P, G, 2]) for u in range(RING)]
        sumsq = [sb(f"sumsq{u}", [P, G]) for u in range(2)]
        vpe = [sb(f"vpe{u}", [P, G]) for u in range(RING)]
        rstd = [sb(f"rstd{u}", [P, G]) for u in range(RING)]
        nmean = [sb(f"nmean{u}", [P, G]) for u in range(RING)]
        shift = [sb(f"shift{u}", [P, G]) for u in range(RING)]
        st3 = [sb(f"st3{u}", [P, G, 6]) for u in range(2)]
        mv3 = [sb(f"mv3{u}", [P, G, 2]) for u in range(2)]
        vpe3 = [sb(f"vpe3{u}", [P, G]) for u in range(2)]
        rstd3 = [sb(f"rstd3{u}", [P, G]) for u in range(2)]
        outT = [sb(f"outT{u}", [P, G * P]) for u in range(2)]
        tln = [sb(f"tln{u}", [P, G, C]) for u in range(2)]
        xn = [sb(f"xn{u}", [P, G, C]) for u in range(2)] + tln
        xt = [sb(f"xt{u}", [P, G, C]) for u in range(2)]
        xh = [sb(f"xh{u}", [P, G, P], F32R) for u in range(2)]
        xl = [sb(f"xl{u}", [P, G, P], F32R) for u in range(2)]
        src = [sb(f"src{u}", [P, TOPK, G, ROW]) for u in range(2)]
        slot = [sb(f"slot{u}", [P, G, TOPK], U32) for u in range(2)]
        mx = sb("mx", [P, G, 8])
        ix = sb("ix", [P, G, 8], U32)
        chosen = sb("chosen", [P, G, TOPK, E])
        picked = sb("picked", [P, G, TOPK, E])
        mask = sb("mask", [P, G + 1, E], BF16)
        th = sb("th", [P, G, E])
        weight = sb("weight", [P, G, TOPK])
        place = sb("place", [P, G, E])
        carry = sb("carry", [P, E])
        pad_row = sb("pad_row", [1, E], I32)
        cnt = sb("cnt", [1, E])
        cnti = sb("cnti", [1, E], I32)
        ntiles_i = sb("ntiles_i", [1, E], I32)
        ntiles = sb("ntiles", [1, E])
        ends8 = sb("ends8", [1, E, E])
        ends = sb("ends", [1, E])
        step_of = sb("step_of", [1, E])
        past = sb("past", [1, SLOTS, E])
        past_s = sb("past_s", [1, SLOTS, E])
        exp_f = sb("exp_f", [1, SLOTS])
        exp_i = sb("exp_i", [1, SLOTS], I32)
        row_f = sb("row_f", [1, SLOTS])
        row_g = sb("row_g", [1, SLOTS])
        row_i = sb("row_i", [1, SLOTS], I32)
        rowt = [sb(f"rowt{v}", [P, ROW]) for v in range(UNROLL)]
        rh = [sb(f"rh{v}", [P, P], F32R) for v in range(4)]
        rl = [sb(f"rl{v}", [P, P], F32R) for v in range(4)]
        sgate = [sb(f"sgate{v}", [P, M]) for v in range(2)]
        hid = [sb(f"hid{v}", [P, M]) for v in range(2)]
        hidT = [sb(f"hidT{v}", [P, MC, P]) for v in range(2)]
        eo = [sb(f"eo{v}", [P, C]) for v in range(4)]
        first_y = X
        second_y = xnT[:].rearrange("p b (t c) -> p b t c", c=C)

        bank = [ctx.enter_context(nc.psum_tensor(f"bank{i}", [P, 512], F32)) for i in range(8)]
        xnT_ps = [bank[0], bank[1], bank[7]]
        S_ps = bank[2:4]
        prep_ps = bank[4]
        chain_ps = [bank[5 + b][:, 0:P] for b in range(B)]
        LT_ps = bank[7][:, 0:P]
        outT_ps, attn_ps, xtT_ps, small_ps = bank[0], bank[1], bank[2], bank[3]
        lg_ps = small_ps[:, 0:G * 2 * E].rearrange("p (i w e) -> p i w e", i=G, w=2)
        pre_ps = small_ps[:, 128:128 + (G + 1) * E].rearrange("p (i e) -> p i e", i=G + 1)
        rowT_ps = bank[0:2]
        z_ps = bank
        gu_ps = bank[4:6]
        hidT_ps = {False: [bank[6][:, 0:M]] * 2, True: [bank[6][:, 0:M], bank[2][:, 0:M]]}
        y_ps = {False: [bank[7][:, 0:C]] * 2, True: [bank[7][:, 0:C], bank[3][:, 0:C]]}

        waits_apart = sem("waits_apart")
        x_in = [sem(f"x_in{n}") for n in range(STEPS)]
        attn_w_in = sem("attn_w_in")
        metric_in = sem("metric_in")
        router_w_in = sem("router_w_in")
        gu_in = sem("gu_in")
        down_in = sem("down_in")
        down_c = sem("down_c")
        zeroed = sem("zeroed")
        consts = sem("consts")
        pool_chain = sem("pool_chain")
        prep_mm = sem("prep_mm")
        prep_sb = sem("prep_sb")
        metric_ready = sem("metric_ready")
        gw_lo_done = sem("gw_lo_done")
        beta_ready = sem("beta_ready")
        gu_hi_done = sem("gu_hi_done")
        gu_lo_done = sem("gu_lo_done")
        st1_w = sem("st1_w")
        mv1_done = sem("mv1_done")
        ln1_c = sem("ln1_c")
        xn_done = sem("xn_done")
        gram_tr = sem("gram_tr")
        xnT_done = sem("xnT_done")
        chain_mm = sem("chain_mm")
        chain_sb = sem("chain_sb")
        gm_done = sem("gm_done")
        outT_mm = sem("outT_mm")
        outT_sb = sem("outT_sb")
        attn_tr = sem("attn_tr")
        sumsq_done = sem("sumsq_done")
        ln2_c = sem("ln2_c")
        x1_done = sem("x1_done")
        st3_w = sem("st3_w")
        mv3_done = sem("mv3_done")
        vpe3_done = sem("vpe3_done")
        ln3_c = sem("ln3_c")
        xt_done = sem("xt_done")
        xtT_tr = sem("xtT_tr")
        xh_done = sem("xh_done")
        xl_done = sem("xl_done")
        logits_mm = sem("logits_mm")
        r1_c = sem("r1_c")
        R1 = 3
        mask_done = sem("mask_done")
        th_done = sem("th_done")
        rb_c = sem("rb_c")
        RB = 2
        prefix_mm = sem("prefix_mm")
        r2_c = sem("r2_c")
        R2 = 3
        src_x_done = sem("src_x_done")
        src_done = sem("src_done")
        rows_out = [sem(f"rows_out{u}") for u in range(2)]
        empty_out = sem("empty_out")
        pads_out = sem("pads_out")
        tab_c = sem("tab_c")
        pad_ready = sem("pad_ready")
        tables = sem("tables")
        gu_mm = sem("gu_mm")
        silu_done = sem("silu_done")
        hid_done = sem("hid_done")
        hidT_tr = sem("hidT_tr")
        hidT_done = sem("hidT_done")
        y_mm = sem("y_mm")
        ysh_done = sem("ysh_done")
        eo_done = sem("eo_done")
        row_in = [sem(f"row_in{v}") for v in range(UNROLL)]
        rowT_tr = sem("rowT_tr")
        rh_done = sem("rh_done")
        rl_done = sem("rl_done")
        res_out = [sem(f"res_out{v}") for v in range(4)]
        y_in = [sem(f"y_in{n}") for n in range(STEPS)]
        z0_done = sem("z0_done")
        z_mm = sem("z_mm")
        sumsq4_done = sem("sumsq4_done")
        ln4_c = sem("ln4_c")
        sum_done = sem("sum_done")
        out_sent = sem("out_sent")

        block = ctx.enter_context(nc.Block())

        def after(eng, s, value):
            if not isinstance(value, int) or value > 0:
                eng.wait_ge(s, value)

        def wait_apart(eng, s, value):
            eng.wait_ge(s, value)
            if not isinstance(value, int):
                eng.sem_inc(waits_apart, 1)

        def back(q, u, d):
            v = (u - d) % 2
            return q - (d - u + v) // 2, v

        def early(q, u):
            return isinstance(q, int) and (q, u) == (1, 0)

        def num(q, u):
            return q * 2 + u

        def exists(q):
            return not isinstance(q, int) or 0 <= q < QS

        def steps(eng, body):
            for u in range(2):
                body(0, u)
            with eng.Fori(1, QS) as q:
                for u in range(2):
                    body(q, u)

        def steps_lagged(eng, body, lag):
            for n in range(3):
                body(n // 2, n % 2)
            with eng.Fori(1, QS - 1) as q:
                body(q, 1)
                body(q + 1, 0)
            for n in range(2 * QS - 1, 2 * QS + lag):
                body(n // 2, n % 2)

        def slots(eng, body, lag):
            for v in range(UNROLL):
                body(0, v)
            with eng.Fori(1, SLOTS // UNROLL - 1) as j:
                for v in range(UNROLL):
                    body(j, v)
            for v in range(UNROLL):
                body(SLOTS // UNROLL - 1, v)
            for v in range(lag):
                body(SLOTS // UNROLL, v)

        def stored(j, v):
            return j * (16 * UNROLL // 4) + (v // 4) * 16 + 16

        def unit_at(j, v):
            return j + v // UNROLL, v % UNROLL

        def tiles(t, q, u):
            return t[:, u, bass.ds(q * G, G)]

        def bc(ap, axis, shape):
            return ap.unsqueeze(axis).to_broadcast(shape)

        @block.sync
        def _(sp):
            for q in range(QS):
                for u in range(B):
                    sp.dma_start(X[:, u, q * G:(q + 1) * G, :],
                                 x_v[:, u, q * G:(q + 1) * G, :]).then_inc(x_in[num(q, u)], 16)
            sp.wait_ge(zeroed, 1)
            sp.dma_start(dcomp[:], diag.rearrange("h (k a) -> (h k) a", a=1),
                         allow_slow_non_contiguous=True).then_inc(metric_in, 16)
            off = 0
            for k in range(K - 1):
                sp.dma_start(ucomp[k:P:K, k + 1:K], halves[:, off:off + K - 1 - k],
                             allow_slow_non_contiguous=True).then_inc(metric_in, 16)
                off += K - 1 - k
            sp.dma_start(gu_f[:, E, 0:M], sg[0]).then_inc(gu_in, 16)
            sp.dma_start(gu_f[:, E, M:2 * M], su[0]).then_inc(gu_in, 16)
            sp.dma_start(gu_f[:, 0:E, 0:M], wg.rearrange("e h m -> h e m")).then_inc(gu_in, 16)
            sp.dma_start(gu_f[:, 0:E, M:2 * M], wu.rearrange("e h m -> h e m")).then_inc(gu_in, 16)
            sp.dma_start(down[:, E, :, :], sd[0].rearrange("(a p) h -> p a h", p=P)).then_inc(down_in, 16)
            for e in range(E):
                sp.dma_start(down[:, e, :, :],
                             wd[e].rearrange("(a p) h -> p a h", p=P)).then_inc(down_in, 16)

            sp.wait_ge(pad_ready, 1)
            for e in range(E):
                row = sp.value_load(pad_row[0:1, e:e + 1], min_val=e * REGION, max_val=e * REGION + T)
                sp.dma_start(rows_d[bass.ds(row, P), :], empty_row[:]).then_inc(pads_out, 16)

            sp.wait_ge(tables, 1)
            for u in range(2):
                sp.wait_ge(rows_out[u], 16 * G * TOPK * QS)
            sp.wait_ge(empty_out, 16)
            sp.wait_ge(pads_out, 16 * E)

            first_row = [sp.alloc_register(f"first_row{v}") for v in range(UNROLL)]

            def load(j, v):
                after(sp, res_out[v % 4], stored(j - 1, v) if not isinstance(j, int) or j > 0 else 0)
                row = sp.snap(first_row[v], min_val=0, max_val=EMPTY_REGION)
                sp.dma_start(rowt[v][:, :], rows_d[bass.ds(row, P), :]).then_inc(row_in[v], 16)

            def loads(j):
                sp.reg_load(first_row, row_i[0:1, bass.ds(j * UNROLL, UNROLL)])
                for v in range(UNROLL):
                    load(j, v)

            loads(0)
            with sp.Fori(1, SLOTS // UNROLL) as j:
                loads(j)

            for v in range(4):
                sp.wait_ge(res_out[v], 16 * SLOTS // 4)

            for q in range(QS):
                for u in range(2):
                    for k, y in enumerate((first_y, second_y)):
                        sp.dma_start(tiles(y, q, u),
                                     res_v[:, k, u * TPB + q * G:u * TPB + (q + 1) * G, :]
                                     ).then_inc(y_in[num(q, u)], 16)

            def output(q, u):
                sp.wait_ge(sum_done, num(q, u) + 1)
                sp.dma_start(tiles(out_v, q, u), tiles(first_y, q, u)).then_inc(out_sent, 16)

            steps(sp, output)
            sp.wait_ge(out_sent, 16 * STEPS)

        @block.gpsimd
        def _(gp):
            done = [0]

            def link(ins):
                done[0] += 1
                ins.then_inc(pool_chain, 1)
                gp.wait_ge(pool_chain, done[0])

            nc.gpsimd.memset(mhalf[:], -0.5)
            nc.gpsimd.memset(ucomp[:], 0.0).then_inc(zeroed, 1)
            link(nc.gpsimd.memset(ident[:], 0.0))
            link(nc.gpsimd.affine_select(out=ident[:], in_=ident[:], compare_op=ALU.not_equal, fill=1.0,
                                         base=0, pattern=[[-1, P]], channel_multiplier=1))
            nc.gpsimd.tensor_scalar(centre[:], ident[:], 1.0 / P, None, ALU.subtract).then_inc(consts, 1)
            link(nc.gpsimd.memset(headmask[:], 1.0))
            link(nc.gpsimd.affine_select(out=headmask[:], in_=headmask[:], compare_op=ALU.is_ge, fill=0.0,
                                         base=0, pattern=[[-K, H], [0, K]], channel_multiplier=1))
            link(nc.gpsimd.affine_select(out=headmask[:], in_=headmask[:], compare_op=ALU.is_ge, fill=0.0,
                                         base=K - 1, pattern=[[K, H], [0, K]], channel_multiplier=-1))
            gp.engine_nop().then_inc(consts, 1)

            def more_constants():
                metric_parts()
                nc.gpsimd.memset(ones_row[:], 1.0)
                nc.gpsimd.memset(beta_row[:, :, 0, :], 0.0)
                nc.gpsimd.memset(ones_b[:], 1.0)
                link(nc.gpsimd.memset(below[:], 1.0))
                link(nc.gpsimd.affine_select(out=below[:], in_=below[:], compare_op=ALU.is_gt, fill=0.0,
                                             base=0, pattern=[[1, P]], channel_multiplier=-1))
                nc.gpsimd.memset(mask[:], 0.0)
                nc.gpsimd.iota(iota8[:], pattern=[[1, E]], base=0, channel_multiplier=0,
                               allow_small_or_imprecise_dtypes=True)
                nc.gpsimd.iota(regbase[:], pattern=[[REGION, E]], base=0, channel_multiplier=0,
                               allow_small_or_imprecise_dtypes=True)
                nc.gpsimd.iota(carry[:], pattern=[[REGION, E]], base=0, channel_multiplier=0,
                               allow_small_or_imprecise_dtypes=True)
                nc.gpsimd.iota(iota_t[:], pattern=[[1, SLOTS]], base=0, channel_multiplier=0,
                               allow_small_or_imprecise_dtypes=True)
                nc.gpsimd.iota(ids[:], pattern=[[T, TOPK], [TPB, B], [1, TPB]], base=0,
                               channel_multiplier=TILES)
                for u in range(2):
                    nc.gpsimd.memset(src[u][:, :, :, P:ROW], 0.0)
                link(nc.gpsimd.memset(upto[:], 1.0))
                link(nc.gpsimd.affine_select(out=upto[:], in_=upto[:], compare_op=ALU.is_ge, fill=0.0,
                                             base=0, pattern=[[1, E], [-1, E]], channel_multiplier=0))
                link(nc.gpsimd.memset(empty_row[:], 0.0))
                link(nc.gpsimd.memset(empty_row[:, P:P + 1].bitcast(I32), NOWHERE))
                nc.gpsimd.dma_start(rows_d[EMPTY_REGION:EMPTY_REGION + P, :], empty_row[:]).then_inc(empty_out, 16)
                gp.wait_ge(router_w_in, 32)
                nc.gpsimd.tensor_copy(beta_row[:, :, 1, :], bc(beta_sb[:], 1, [1, G, E])).then_inc(beta_ready, 1)
                gp.wait_ge(prep_sb, 2)
                nc.gpsimd.tensor_tensor(gw_lo[:], bc(gwT[:], 1, [P, 2, E]), gw_hi[:].bitcast(F32),
                                        ALU.subtract).then_inc(gw_lo_done, 1)
                gp.engine_nop().then_inc(consts, 1)

            def metric_parts():
                gp.wait_ge(metric_in, 16 * K)
                nc.gpsimd.tensor_tensor(ubig[:].rearrange("p (h k) -> p h k", h=H),
                                        bc(ucomp[:], 1, [P, H, K]), headmask[:], ALU.mult)
                link(nc.gpsimd.tensor_scalar(iddiag[:], ident[:], dcomp[:], None, ALU.mult))
                nc.gpsimd.tensor_tensor(udiag[:], ubig[:], iddiag[:], ALU.add).then_inc(metric_ready, 1)

            def norm(var, factor, vpe_u, rstd_u, s, base):
                nc.gpsimd.tensor_scalar(vpe_u[:], var, factor, EPS, ALU.mult, ALU.add).then_inc(s, 1)
                gp.wait_ge(s, base + 1)
                nc.gpsimd.tensor_tensor(rstd_u[:], vpe_u[:], mhalf[:], ALU.pow).then_inc(s, 1)

            def norm_shift(mv_u, vpe_u, rstd_u, nmean_u, shift_u, s, base):
                nc.gpsimd.tensor_scalar(nmean_u[:], mv_u[:, :, 0], -1.0, None, ALU.mult).then_inc(s, 1)
                norm(mv_u[:, :, 1], 1.0, vpe_u, rstd_u, s, base + 1)
                gp.wait_ge(s, base + 3)
                nc.gpsimd.tensor_tensor(shift_u[:], nmean_u[:], rstd_u[:], ALU.mult).then_inc(s, 1)

            for s in range(STEPS):
                r = s % RING
                after(gp, xn_done, s - RING + 1)
                gp.wait_ge(mv1_done, s + 1)
                norm_shift(mv[r], vpe[r], rstd[r], nmean[r], shift[r], ln1_c, s * 4)
            more_constants()

            def scatter(q, u, i):
                for k in range(TOPK):
                    nc.gpsimd.indirect_dma_start(
                        rows_d, bass.IndirectOffsetOnAxis(ap=slot[u][:, i, k:k + 1], axis=0),
                        src[u][:, k, i, :], None).then_inc(rows_out[u], 16)

            def ready_rows(q, u):
                wait_apart(gp, src_x_done, num(q, u) + 1)
                wait_apart(gp, src_done, num(q, u) + 1)

            def attn_step(q, u):
                q1, u1 = back(q, u, 1)
                q2, u2 = back(q, u, 2)
                q3, u3 = back(q, u, 3)
                if exists(q1):
                    gp.wait_ge(vpe3_done, num(q1, u1) + 1)
                    nc.gpsimd.tensor_tensor(rstd3[u1][:], vpe3[u1][:], mhalf[:], ALU.pow).then_inc(ln3_c, 1)
                if exists(q3):
                    scatter(q3, u3, 2)
                    scatter(q3, u3, 3)
                if exists(q):
                    wait_apart(gp, sumsq_done, num(q, u) + 1)
                    norm(sumsq[u][:], 1.0 / P, vpe[u], rstd[u], ln2_c, num(q, u) * 2)
                if exists(q2):
                    ready_rows(q2, u2)
                    scatter(q2, u2, 0)
                    scatter(q2, u2, 1)

            steps_lagged(gp, attn_step, 3)

            def store(j, v):
                wait_apart(gp, eo_done, j * UNROLL + v + 1)
                nc.gpsimd.indirect_dma_start(
                    res_d, bass.IndirectOffsetOnAxis(ap=rowt[v][:, P:P + 1].bitcast(U32), axis=0),
                    eo[v % 4][:], None, bounds_check=TOPK * T - 1, oob_is_err=False
                ).then_inc(res_out[v % 4], 16)

            slots(gp, store, 0)

            for n in range(STEPS):
                u = n % 2
                after(gp, sum_done, n - 1)
                gp.wait_ge(sumsq4_done, n + 1)
                norm(sumsq[u][:], 1.0 / P, vpe[u], rstd[u], ln4_c, n * 2)

        def silu(act, g, v):
            act.wait_ge(gu_mm, g + 1)
            after(act, hid_done, g - 1)
            nc.scalar.activation(sgate[v][:], gu_ps[v][:, 0:M], ACT.Silu).then_inc(silu_done, 1)

        def hidT_copy(act, g, v, own=False):
            if isinstance(g, int) and g < 0:
                return
            act.wait_ge(hidT_tr, g + 1)
            after(act, y_mm, g - 1)
            nc.scalar.activation(hidT[v][:].rearrange("p a t -> p (a t)"), hidT_ps[own][v],
                                 ACT.Copy).then_inc(hidT_done, 1)

        @block.scalar
        def _(act):
            act.dma_start(Wc[:], proj[0].rearrange("n c k -> c n k")).then_inc(attn_w_in, 16)
            act.dma_start(mix[:], mixer_w).then_inc(attn_w_in, 16)
            act.dma_start(mixb[:], mixer_b.rearrange("(c a) -> c a", a=1), allow_slow_non_contiguous=True).then_inc(attn_w_in, 16)
            act.dma_start(gw[:], gate_w).then_inc(router_w_in, 16)
            act.dma_start(beta_sb[:], beta.rearrange("(a e) -> a e", a=1)).then_inc(router_w_in, 16)
            act.wait_ge(zeroed, 1)
            nc.scalar.activation(table_in[:], mhalf[:], ACT.Silu)

            for s in range(STEPS):
                r = s % RING
                act.wait_ge(ln1_c, s * 4 + 4)
                after(act, gram_tr, s - RING + 1)
                for i in range(G):
                    last = nc.scalar.activation(xn[r][:, i, :], X[:, s % 2, s // 2 * G + i, :],
                                                ACT.Identity, bias=shift[r][:, i:i + 1], scale=rstd[r][:, i:i + 1])
                last.then_inc(xn_done, 1)

            act.wait_ge(prep_mm, 1)
            nc.scalar.activation(WT[:], prep_ps[:, 0:128], ACT.Copy)
            nc.scalar.activation(mixT[:], prep_ps[:, 128:256], ACT.Copy)
            nc.scalar.activation(mixb_c[:], prep_ps[:, 256 + E:257 + E], ACT.Copy)
            nc.scalar.activation(gwT[:], prep_ps[:, 256:256 + E], ACT.Copy).then_inc(prep_sb, 1)
            act.wait_ge(prep_sb, 1)
            nc.scalar.activation(gw_hi[:], bc(gwT[:], 1, [P, 2, E]), ACT.Copy).then_inc(prep_sb, 1)

            act.wait_ge(gram_tr, STEPS)
            for b in range(B):
                nc.scalar.activation(S_sb[b][:], S_ps[b][:, 0:P], ACT.Copy).then_inc(chain_sb, 1)
            for n, dst in ((0, T1), (2, R_sb), (3, A_sb)):
                for b in range(B):
                    act.wait_ge(chain_mm, n * B + b + 1)
                    nc.scalar.activation(dst[b][:], chain_ps[b], ACT.Copy).then_inc(chain_sb, 1)
                if dst is T1:
                    act.wait_ge(prep_mm, 3)
                    nc.scalar.activation(LT[:], LT_ps, ACT.Copy).then_inc(prep_sb, 1)

            def high(e):
                nc.scalar.activation(gu_hi[:, e, :], gu_f[:, e, :], ACT.Copy).then_inc(gu_hi_done, 1)

            act.wait_ge(gu_in, 64)
            high(E)

            def unit(q, u, i):
                g = num(q, u) * G + i
                silu(act, g, i % 2)
                hidT_copy(act, g - 1, (i - 1) % 2)
                ysh_copy(q, u, i - 2)

            def ysh_copy(q, u, i):
                if i < 0:
                    q, u = back(q, u, 1)
                    i += G
                    if not exists(q):
                        return
                g = num(q, u) * G + i
                act.wait_ge(y_mm, g + 1)
                nc.scalar.activation(ysh[:, u, bass.ds(q * G + i, 1), :].rearrange("p a c -> p (a c)"),
                                     y_ps[False][i % 2], ACT.Copy).then_inc(ysh_done, 1)

            def attention_T(q, u):
                s = num(q, u)
                act.wait_ge(outT_mm, s + 1)
                after(act, attn_tr, s - 1)
                nc.scalar.activation(outT[u][:], outT_ps[:, :], ACT.Identity, bias=mixb_c[:]).then_inc(outT_sb, 1)

            def attn_step(q, u):
                q1, u1 = back(q, u, 1)
                q2, u2 = back(q, u, 2)
                s = num(q, u)
                s1 = num(q1, u1)
                if exists(q):
                    attention_T(q, u)
                if exists(q2):
                    unit(q2, u2, 1)
                if exists(q):
                    act.wait_ge(attn_tr, s + 1)
                    after(act, ln2_c, (s - 1) * 2)
                    for i in range(G):
                        last = nc.scalar.activation(tln[u][:, i, :], attn_ps[:, i * P:(i + 1) * P], ACT.Square,
                                                    accum_out=sumsq[u][:, i:i + 1])
                    last.then_inc(sumsq_done, 1)
                if exists(q2):
                    unit(q2, u2, 2)
                if exists(q1):
                    act.wait_ge(xtT_tr, s1 + 1)
                    after(act, gu_mm, (s1 - 1) * G)
                    nc.scalar.activation(xh[u1][:].rearrange("p i t -> p (i t)"), xtT_ps[:, :],
                                         ACT.Copy).then_inc(xh_done, 1)
                if exists(q2):
                    unit(q2, u2, 3)
                if exists(q1):
                    act.wait_ge(logits_mm, s1 + 1)
                    after(act, rb_c, s1 * RB)
                    nc.scalar.activation(th[:], lg_ps[:, :, 0, :], ACT.Tanh, scale=0.5).then_inc(th_done, 1)
                    unit(q1, u1, 0)
                    after(act, rows_out[u1], q1 * 16 * G * TOPK)
                    for k in range(TOPK):
                        last = nc.scalar.activation(src[u1][:, k, :, 0:P], xt[u1][:], ACT.Copy)
                    last.then_inc(src_x_done, 1)

            steps_lagged(act, attn_step, 2)
            hidT_copy(act, TILES - 1, 1)
            ysh_copy(QS - 1, 1, 2)
            ysh_copy(QS - 1, 1, 3)
            for e in range(E):
                high(e)

            def row_high(j, v):
                r = j * UNROLL + v
                act.wait_ge(rowT_tr, r + 1)
                after(act, gu_mm, r - 4 + TILES + 1)
                nc.scalar.activation(rh[v % 4][:], rowT_ps[v % 2][:, 0:P], ACT.Copy).then_inc(rh_done, 1)

            def routed(j, v):
                r = j * UNROLL + v
                if not isinstance(r, int) or r < SLOTS:
                    silu(act, r + TILES, v % 2)
                if not isinstance(r, int) or r + 2 < SLOTS:
                    row_high(*unit_at(j, v + 2))
                if not isinstance(r, int) or 1 <= r <= SLOTS:
                    hidT_copy(act, r - 1 + TILES, (v - 1) % 2, True)

            row_high(0, 0)
            row_high(0, 1)
            slots(act, routed, 1)

            for n in range(STEPS):
                u = n % 2
                act.wait_ge(z_mm, n + 1)
                after(act, ln4_c, (n - 1) * 2)
                for i in range(G):
                    last = nc.scalar.activation(tln[u][:, i, :], z_ps[n][:, i * P:(i + 1) * P], ACT.Square,
                                                accum_out=sumsq[u][:, i:i + 1])
                last.then_inc(sumsq4_done, 1)

        @block.vector
        def _(dve):
            def stats(src_of, st_u, mv_u, st_sem, mv_sem, s):
                for i in range(G):
                    last = nc.vector.bn_stats(st_u[:, i, :], src_of(i))
                last.then_inc(st_sem, 1)
                wait_apart(dve, st_sem, s + 1)
                for i in range(G):
                    last = nc.vector.bn_aggr(mv_u[:, i, :], st_u[:, i, :])
                last.then_inc(mv_sem, 1)

            def xnT_copy(s):
                dve.wait_ge(gram_tr, s + 1)
                nc.vector.tensor_copy(xnT[:, s % 2, s // 2 * G * P:(s // 2 + 1) * G * P],
                                      xnT_ps[s % 3][:, :]).then_inc(xnT_done, 1)

            def make_metric():
                dve.wait_ge(metric_ready, 1)
                dve.wait_ge(prep_mm, 2)
                nc.vector.tensor_tensor(metric[:], prep_ps[:, 384:512], udiag[:], ALU.add).then_inc(metric_ready, 1)

            for s in range(STEPS + 4):
                if s < STEPS:
                    r = s % RING
                    dve.wait_ge(x_in[s], 16)
                    after(dve, ln1_c, (s - RING + 1) * 4)
                    stats(lambda i: X[:, s % 2, s // 2 * G + i, :], st[r], mv[r], st1_w, mv1_done, s)
                if s >= 4:
                    xnT_copy(s - 4)
            make_metric()
            dve.wait_ge(consts, 2)
            for b in range(B):
                dve.wait_ge(chain_mm, B + b + 1)
                nc.vector.tensor_tensor(Gm[b][:], chain_ps[b], headmask[:].rearrange("p h k -> p (h k)"),
                                        ALU.mult).then_inc(gm_done, 1)

            def low(n, e):
                dve.wait_ge(gu_hi_done, n + 1)
                nc.vector.tensor_tensor(gu_lo[:, e, :], gu_f[:, e, :], gu_hi[:, e, :].bitcast(F32),
                                        ALU.subtract).then_inc(gu_lo_done, 1)

            low(0, E)

            dve.wait_ge(down_in, 16 * (E + 1))
            nc.vector.tensor_reduce(down_mean[:], down[:], axis=AX.X, op=ALU.add).then_inc(down_c, 1)
            dve.wait_ge(down_c, 1)
            nc.vector.tensor_scalar(down_mean[:], down_mean[:], 1.0 / C, None, ALU.mult).then_inc(down_c, 1)
            dve.wait_ge(consts, 3)

            def centre_down():
                dve.wait_ge(down_c, 2)
                nc.vector.tensor_tensor(down[:], down[:], bc(down_mean[:], 3, [P, E + 1, MC, C]),
                                        ALU.subtract).then_inc(down_c, 1)

            def hidden(g, v):
                dve.wait_ge(silu_done, g + 1)
                after(dve, hidT_tr, g - 1)
                nc.vector.tensor_tensor(hid[v][:], sgate[v][:], gu_ps[v][:, M:2 * M], ALU.mult).then_inc(hid_done, 1)

            def normalise(q, u):
                s = num(q, u)
                dve.wait_ge(ln3_c, s + 1)
                after(dve, src_x_done, s - 1)
                for i in range(G):
                    last = nc.vector.tensor_scalar(xt[u][:, i, :], x1[:, u, bass.ds(q * G + i, 1), :].rearrange("p a c -> p (a c)"),
                                                   mv3[u][:, i, 0:1], rstd3[u][:, i:i + 1], ALU.subtract, ALU.mult)
                last.then_inc(xt_done, 1)

            def low_part(q, u):
                dve.wait_ge(xh_done, num(q, u) + 1)
                nc.vector.tensor_tensor(xl[u][:].rearrange("p i t -> p (i t)"), xtT_ps[:, :],
                                        xh[u][:].rearrange("p i t -> p (i t)").bitcast(F32),
                                        ALU.subtract).then_inc(xl_done, 1)

            def choose(q, u):
                s = num(q, u)
                n = [0]

                def link(ins):
                    n[0] += 1
                    ins.then_inc(r1_c, 1)
                    wait_apart(dve, r1_c, s * R1 + n[0])

                wait_apart(dve, th_done, s + 1)
                for i in range(G):
                    last = nc.vector.max(mx[:, i, :], lg_ps[:, i, 1, :])
                link(last)
                for i in range(G):
                    last = nc.vector.max_index(ix[:, i, :], mx[:, i, :], lg_ps[:, i, 1, :])
                link(last)
                link(nc.vector.tensor_tensor(chosen[:], iota8[:].unsqueeze(1).unsqueeze(1).to_broadcast([P, G, TOPK, E]),
                                             bc(ix[:, :, 0:TOPK], 3, [P, G, TOPK, E]), ALU.is_equal))
                assert n[0] == R1
                after(dve, prefix_mm, s)
                nc.vector.tensor_tensor(mask[:, 0:G, :], chosen[:, :, 0, :], chosen[:, :, 1, :],
                                        ALU.add).then_inc(mask_done, 1)

            def probabilities(q, u):
                s = num(q, u)
                nc.vector.tensor_tensor(picked[:], chosen[:], bc(th[:], 2, [P, G, TOPK, E]),
                                        ALU.mult).then_inc(rb_c, 1)
                dve.wait_ge(rb_c, s * RB + 1)
                nc.vector.tensor_reduce(weight[:], picked[:], axis=AX.X, op=ALU.add).then_inc(rb_c, 1)

            def places(q, u):
                s = num(q, u)
                dve.wait_ge(prefix_mm, s + 1)
                nc.vector.tensor_tensor(place[:], pre_ps[:, 0:G, :], bc(carry[:], 1, [P, G, E]),
                                        ALU.add).then_inc(r2_c, 1)
                dve.wait_ge(rb_c, s * RB + RB)
                after(dve, rows_out[u], q * 16 * G * TOPK)
                nc.vector.tensor_scalar(src[u][:, :, :, P + 1:P + 2].rearrange("p k i a -> p k (i a)"),
                                        weight[:].rearrange("p i k -> p k i"), 0.5, 0.5, ALU.mult, ALU.add)
                dve.wait_ge(r2_c, s * R2 + 1)
                nc.vector.tensor_tensor(picked[:], chosen[:], bc(place[:], 2, [P, G, TOPK, E]),
                                        ALU.mult).then_inc(r2_c, 1)
                nc.vector.tensor_copy(src[u][:, :, :, P:P + 1].rearrange("p k i a -> p k (i a)").bitcast(I32),
                                      ids[:, :, u, bass.ds(q * G, G)])
                dve.wait_ge(r2_c, s * R2 + 2)
                nc.vector.tensor_tensor(carry[:], carry[:], pre_ps[:, G, :], ALU.add).then_inc(r2_c, 1)
                with nc.allow_low_precision(reason="whole numbers below 2 ** 24"):
                    nc.vector.tensor_reduce(slot[u][:], picked[:], axis=AX.X, op=ALU.add).then_inc(src_done, 1)
                dve.wait_ge(r2_c, s * R2 + R2)

            def attn_step(q, u):
                q1, u1 = back(q, u, 1)
                q2, u2 = back(q, u, 2)
                if early(q, u):
                    places(q2, u2)
                if exists(q1):
                    normalise(q1, u1)
                if exists(q2):
                    hidden(num(q2, u2) * G + 1, 1)
                    if not early(q, u):
                        places(q2, u2)
                    hidden(num(q2, u2) * G + 2, 0)
                if exists(q1):
                    low_part(q1, u1)
                if isinstance(q, int) and (q, u) == (0, 1):
                    centre_down()
                if exists(q2):
                    hidden(num(q2, u2) * G + 3, 1)
                if exists(q):
                    s = num(q, u)
                    dve.wait_ge(ln2_c, s * 2 + 2)
                    for i in range(G):
                        tile = bass.ds(q * G + i, 1)
                        last = nc.vector.scalar_tensor_tensor(
                            out=x1[:, u, tile, :].rearrange("p a c -> p (a c)"), in0=attn_ps[:, i * P:(i + 1) * P],
                            scalar=rstd[u][:, i:i + 1], in1=X[:, u, tile, :].rearrange("p a c -> p (a c)"),
                            op0=ALU.mult, op1=ALU.add)
                    last.then_inc(x1_done, 1)
                    wait_apart(dve, x1_done, s + 1)
                    stats(lambda i: x1[:, u, bass.ds(q * G + i, 1), :].rearrange("p a c -> p (a c)"),
                          st3[u], mv3[u], st3_w, mv3_done, s)
                    wait_apart(dve, mv3_done, s + 1)
                    nc.vector.tensor_scalar(vpe3[u][:], mv3[u][:, :, 1], EPS, None, ALU.add).then_inc(vpe3_done, 1)
                if exists(q1):
                    choose(q1, u1)
                    probabilities(q1, u1)
                    hidden(num(q1, u1) * G, 0)

            steps_lagged(dve, attn_step, 2)

            n = [0]

            def link(ins):
                n[0] += 1
                ins.then_inc(tab_c, 1)
                dve.wait_ge(tab_c, n[0])

            nc.vector.tensor_copy(pad_row[:], carry[0:1, :]).then_inc(pad_ready, 1)
            link(nc.vector.tensor_tensor(cnt[:], carry[0:1, :], regbase[0:1, :], ALU.subtract))
            link(nc.vector.tensor_scalar(cnti[:], cnt[:], float(P - 1), None, ALU.add))
            link(nc.vector.tensor_scalar(ntiles_i[:], cnti[:], 7, None, ALU.logical_shift_right))
            link(nc.vector.tensor_copy(ntiles[:], ntiles_i[:]))
            nc.vector.tensor_scalar(step_of[:], ntiles[:], float(-P), float(REGION), ALU.mult, ALU.add)
            link(nc.vector.tensor_tensor(ends8[:], upto[:], bc(ntiles[:], 1, [1, E, E]), ALU.mult))
            link(nc.vector.tensor_reduce(ends[:], ends8[:], axis=AX.X, op=ALU.add))
            link(nc.vector.tensor_tensor(past[:], bc(iota_t[:], 2, [1, SLOTS, E]), bc(ends[:], 1, [1, SLOTS, E]),
                                         ALU.is_ge))
            nc.vector.tensor_tensor(past_s[:], past[:], bc(step_of[:], 1, [1, SLOTS, E]), ALU.mult)
            link(nc.vector.tensor_reduce(exp_f[:], past[:], axis=AX.X, op=ALU.add))
            nc.vector.tensor_scalar(exp_i[:], exp_f[:], float(E - 1), None, ALU.min)
            link(nc.vector.tensor_reduce(row_f[:], past_s[:], axis=AX.X, op=ALU.add))
            link(nc.vector.scalar_tensor_tensor(out=row_g[:], in0=iota_t[:], scalar=float(P), in1=row_f[:],
                                                op0=ALU.mult, op1=ALU.add))
            nc.vector.tensor_scalar(row_i[:], row_g[:], float(EMPTY_REGION), None, ALU.min).then_inc(tables, 1)

            for e in range(E):
                low(e + 1, e)

            def row_low(j, v):
                dve.wait_ge(rh_done, j * UNROLL + v + 1)
                nc.vector.tensor_tensor(rl[v % 4][:], rowT_ps[v % 2][:, 0:P], rh[v % 4][:].bitcast(F32),
                                        ALU.subtract).then_inc(rl_done, 1)

            def routed(j, v):
                r = j * UNROLL + v
                if not isinstance(r, int) or r < SLOTS:
                    hidden(r + TILES, v % 2)
                if not isinstance(r, int) or r + 2 < SLOTS:
                    row_low(*unit_at(j, v + 2))
                if not isinstance(r, int) or r >= 2:
                    jw, w = unit_at(j, v - 2)
                    dve.wait_ge(y_mm, r - 2 + TILES + 1)
                    if not isinstance(r, int) or r >= 6:
                        dve.wait_ge(res_out[w % 4], stored(*unit_at(j, v - 6)))
                    nc.vector.tensor_scalar(eo[w % 4][:], y_ps[True][w % 2], rowt[w][:, P + 1:P + 2], None,
                                            ALU.mult).then_inc(eo_done, 1)

            row_low(0, 0)
            row_low(0, 1)
            slots(dve, routed, 2)

            for n in range(STEPS + 3):
                if n < STEPS:
                    q, u = n // 2, n % 2
                    dve.wait_ge(y_in[n], 16 * TOPK)
                    nc.vector.tensor_tensor(tiles(first_y, q, u), tiles(first_y, q, u), tiles(second_y, q, u),
                                            ALU.add).then_inc(z0_done, 1)
                if n >= 3:
                    s = n - 3
                    q, u = s // 2, s % 2
                    dve.wait_ge(ln4_c, s * 2 + 2)
                    for i in range(G):
                        last = nc.vector.scalar_tensor_tensor(
                            out=first_y[:, u, q * G + i, :], in0=z_ps[s][:, i * P:(i + 1) * P],
                            scalar=rstd[u][:, i:i + 1], in1=x1[:, u, q * G + i, :], op0=ALU.mult, op1=ALU.add)
                    last.then_inc(sum_done, 1)

        @block.tensor
        def _(pe):
            mm = nc.tensor.matmul
            pe.wait_ge(consts, 1)

            for s in range(STEPS):
                if s == 2:
                    Wf = Wc[:].rearrange("p h k -> p (h k)")
                    pe.wait_ge(attn_w_in, 48)
                    pe.wait_ge(router_w_in, 32)
                    nc.tensor.transpose(prep_ps[:, 0:128], Wf, ident[:])
                    mm(prep_ps[:, 128:256], mix[:], centre[:], start=True, stop=True)
                    nc.tensor.transpose(prep_ps[:, 256:256 + E], gw[:], ident[0:E, 0:E])
                    mm(prep_ps[:, 256 + E:257 + E], centre[:], mixb[:], start=True, stop=True).then_inc(prep_mm, 1)
                pe.wait_ge(xn_done, s + 1)
                after(pe, xnT_done, s - 2)
                x_n = xn[s % RING]
                for i in range(G):
                    mm(S_ps[s % 2][:, 0:P], x_n[:, i, :], x_n[:, i, :], start=s < 2 and i == 0,
                       stop=i == G - 1, skip_group_check=True)
                for i in range(G):
                    last = nc.tensor.transpose(xnT_ps[s % 3][:, i * P:(i + 1) * P], x_n[:, i, :], ident[:])
                last.then_inc(gram_tr, 1)

            def chain(left, right, ready, at):
                for b in range(B):
                    pe.wait_ge(ready, at + b + 1)
                    mm(chain_ps[b], left(b), right(b), start=True, stop=True).then_inc(chain_mm, 1)

            pe.wait_ge(prep_sb, 1)
            chain(lambda b: S_sb[b][:], lambda b: Wf, chain_sb, 0)
            pe.wait_ge(metric_ready, 1)
            nc.tensor.transpose(prep_ps[:, 384:512], ubig[:], ident[:]).then_inc(prep_mm, 1)
            pe.wait_ge(metric_ready, 2)
            pe.wait_ge(xnT_done, STEPS - 2)
            mm(LT_ps, metric[:], WT[:], start=True, stop=True).then_inc(prep_mm, 1)
            chain(lambda b: Wf, lambda b: T1[b][:], chain_sb, B)
            pe.wait_ge(prep_sb, 3)
            chain(lambda b: Gm[b][:], lambda b: mixT[:], gm_done, 0)
            chain(lambda b: LT[:], lambda b: R_sb[b][:], chain_sb, 2 * B)
            pe.wait_ge(chain_sb, 4 * B)
            pe.wait_ge(xnT_done, STEPS)

            def gate_up(g, v, hi, lo, e):
                after(pe, hid_done, g - 1)
                mm(gu_ps[v][:, :], hi, gu_hi[:, e, :], start=True, stop=False)
                mm(gu_ps[v][:, :], hi, gu_lo[:, e, :], start=False, stop=False)
                mm(gu_ps[v][:, :], lo, gu_hi[:, e, :], start=False, stop=True).then_inc(gu_mm, 1)

            def hidden_T(g, v, own=False):
                if isinstance(g, int) and g < 0:
                    return
                pe.wait_ge(hid_done, g + 1)
                after(pe, hidT_done, g - 1 if own else g)
                for a in range(MC):
                    last = nc.tensor.transpose(hidT_ps[own][v][:, a * P:(a + 1) * P], hid[v][:, a * P:(a + 1) * P], ident[:])
                last.then_inc(hidT_tr, 1)

            def result(g, v, e, own=False):
                if isinstance(g, int) and g == 0:
                    pe.wait_ge(down_c, 3)
                pe.wait_ge(hidT_done, g + 1)
                for a in range(MC):
                    last = mm(y_ps[own][v], hidT[v][:, a, :], down[:, e, a, :], start=a == 0, stop=a == MC - 1)
                last.then_inc(y_mm, 1)

            def shared(q, u, i):
                g = num(q, u) * G + i
                gate_up(g, i % 2, xh[u][:, i, :], xl[u][:, i, :], E)
                hidden_T(g - 1, (i - 1) % 2)
                if not isinstance(g, int) or g >= 2:
                    after(pe, ysh_done, g - 2)
                    result(g - 2, i % 2, E)

            def attention_T(q, u):
                s = num(q, u)
                after(pe, outT_sb, s)
                mm(outT_ps[:, :], A_sb[u][:], xnT[:, u, bass.ds(q * G * P, G * P)], start=True,
                   stop=True).then_inc(outT_mm, 1)

            def attention(q, u):
                s = num(q, u)
                pe.wait_ge(outT_sb, s + 1)
                after(pe, x1_done, s)
                for i in range(G):
                    last = nc.tensor.transpose(attn_ps[:, i * P:(i + 1) * P], outT[u][:, i * P:(i + 1) * P], ident[:])
                last.then_inc(attn_tr, 1)

            def prefix(q, u):
                pe.wait_ge(mask_done, num(q, u) + 1)
                mm(pre_ps, below[:], mask[:], start=True, stop=False)
                for i in range(G):
                    last = mm(pre_ps[:, i + 1:G + 1, :], ones_b[:], bc(mask[:, i, :], 1, [P, G - i, E]),
                              start=False, stop=i == G - 1)
                last.then_inc(prefix_mm, 1)

            def attn_step(q, u):
                q1, u1 = back(q, u, 1)
                q2, u2 = back(q, u, 2)
                s1 = num(q1, u1)
                if exists(q):
                    attention_T(q, u)
                if early(q, u):
                    prefix(q2, u2)
                if exists(q2):
                    shared(q2, u2, 1)
                    if not early(q, u):
                        prefix(q2, u2)
                if exists(q):
                    attention(q, u)
                if exists(q2):
                    shared(q2, u2, 2)
                if exists(q1):
                    pe.wait_ge(xt_done, s1 + 1)
                    after(pe, xl_done, s1)
                    for i in range(G):
                        last = nc.tensor.transpose(xtT_ps[:, i * P:(i + 1) * P], xt[u1][:, i, :], ident[:])
                    last.then_inc(xtT_tr, 1)
                if exists(q2):
                    shared(q2, u2, 3)
                if exists(q1):
                    if isinstance(s1, int) and s1 == 0:
                        pe.wait_ge(gw_lo_done, 1)
                        pe.wait_ge(beta_ready, 1)
                        pe.wait_ge(gu_lo_done, 1)
                        pe.wait_ge(consts, 3)
                    after(pe, r2_c, s1 * R2)
                    mm(small_ps[:, 0:G * 2 * E], ones_row[:], beta_row[:].rearrange("a i w e -> a (i w e)"),
                       start=True, stop=False, skip_group_check=True)
                    pe.wait_ge(xl_done, s1 + 1)
                    for i in range(G):
                        for x_part, w_part in ((xh, gw_hi), (xh, gw_lo), (xl, gw_hi), (xl, gw_lo)):
                            last = mm(lg_ps[:, i].rearrange("p w e -> p (w e)"), x_part[u1][:, i, :],
                                      w_part[:].rearrange("p w e -> p (w e)"), start=False,
                                      stop=w_part is gw_lo and x_part is xl, skip_group_check=True)
                    last.then_inc(logits_mm, 1)
                    shared(q1, u1, 0)

            steps_lagged(pe, attn_step, 2)
            hidden_T(TILES - 1, 1)
            pe.wait_ge(ysh_done, TILES - 2)
            result(TILES - 2, 0, E)
            pe.wait_ge(ysh_done, TILES - 1)
            result(TILES - 1, 1, E)
            pe.wait_ge(ysh_done, TILES)

            pe.wait_ge(tables, 1)
            pe.wait_ge(gu_lo_done, E + 1)

            def row_T(j, v):
                pe.wait_ge(row_in[v], j * 16 + 16)
                after(pe, rl_done, j * UNROLL + v - 1)
                nc.tensor.transpose(rowT_ps[v % 2][:, 0:P], rowt[v][:, 0:P], ident[:]).then_inc(rowT_tr, 1)

            own = [pe.alloc_register(f"expert{k}") for k in range(UNROLL + 2)]
            coming = [pe.alloc_register(f"next_expert{k}") for k in range(UNROLL)]

            def expert(v):
                return bass.ds(pe.snap(own[v + 2], min_val=0, max_val=E - 1), 1)

            def block_turns(j):
                for k in range(2):
                    pe.reg_mov(own[k], own[UNROLL + k])
                for k in range(UNROLL):
                    pe.reg_mov(own[k + 2], coming[k])

            def routed(j, v):
                r = j * UNROLL + v
                if not isinstance(r, int) or r < SLOTS:
                    e = expert(v)
                    pe.wait_ge(rl_done, r + 1)
                    gate_up(r + TILES, v % 2, rh[v % 4][:], rl[v % 4][:], e)
                if not isinstance(r, int) or r + 2 < SLOTS:
                    row_T(*unit_at(j, v + 2))
                if v == 4 and (not isinstance(j, int) or j + 1 < SLOTS // UNROLL):
                    pe.reg_load(coming, exp_i[0:1, bass.ds((j + 1) * UNROLL, UNROLL)])
                if not isinstance(r, int) or 1 <= r <= SLOTS:
                    hidden_T(r - 1 + TILES, (v - 1) % 2, True)
                if not isinstance(r, int) or r >= 2:
                    e = expert(v - 2)
                    after(pe, eo_done, r - 3)
                    result(r - 2 + TILES, v % 2, e, True)

            def block_of(j, n):
                block_turns(j)
                for v in range(n):
                    routed(j, v)

            row_T(0, 0)
            row_T(0, 1)
            for k in range(2):
                pe.reg_mov(own[UNROLL + k], 0)
            pe.reg_load(coming, exp_i[0:1, 0:UNROLL])
            block_of(0, UNROLL)
            with pe.Fori(1, SLOTS // UNROLL - 1) as j:
                block_of(j, UNROLL)
            block_of(SLOTS // UNROLL - 1, UNROLL)
            routed(SLOTS // UNROLL - 1, UNROLL)
            routed(SLOTS // UNROLL - 1, UNROLL + 1)

            pe.wait_ge(hid_done, SLOTS + TILES)
            pe.wait_ge(hidT_done, SLOTS + TILES)
            pe.wait_ge(eo_done, SLOTS)
            for n in range(STEPS):
                mm(z_ps[n][:, :], ident[:], tiles(ysh, n // 2, n % 2).rearrange("p i c -> p (i c)"),
                   start=True, stop=False)
            for n in range(STEPS):
                pe.wait_ge(z0_done, n + 1)
                mm(z_ps[n][:, :], ident[:], tiles(first_y, n // 2, n % 2).rearrange("p i c -> p (i c)"),
                   start=False, stop=True).then_inc(z_mm, 1)


_INS = ["L0_attn_in_sequence_bwc", "L0_attn_projection_1nck", "L0_attn_halves", "L0_attn_diagonals_nk",
        "L0_attn_mixer_w", "L0_attn_mixer_b", "L0_ffn_gate_w", "L0_ffn_beta", "L0_ffn_gate_proj_w",
        "L0_ffn_up_proj_w", "L0_ffn_down_proj_w", "L0_ffn_shared_gate_w", "L0_ffn_shared_up_w",
        "L0_ffn_shared_down_w"]


def kernel(**inputs):
    import numpy as np
    import concourse.bacc as bacc
    from concourse.bass_utils import run_bass_kernel_spmd

    nc = bacc.Bacc("TRN2", target_bir_lowering=False, num_devices=1)
    arrays, args = {}, []
    for name in _INS:
        a = np.ascontiguousarray(inputs[name])
        arrays[f"in_{name}"] = a
        args.append(nc.dram_tensor(f"in_{name}", a.shape, mybir.dt.from_np(a.dtype), kind="ExternalInput").ap())
    shape = inputs[_INS[0]].shape
    args.append(nc.dram_tensor("out_0", shape, F32, kind="ExternalOutput").ap())
    build_sandwich(nc, *args)
    r = run_bass_kernel_spmd(nc, [arrays], core_ids=[0])
    return r.results[0]["out_0"]
```
